# Optimizing a Trainium2 kernel written in Bass

```python
import numpy as np
import jax
import jax.numpy as jnp

def _softmax(x, axis=-1):
    return jax.nn.softmax(x, axis=axis)
def _gelu(x):
    return jax.nn.gelu(x, approximate=True)
def _silu(x):
    return jax.nn.silu(x)
def _sigmoid(x):
    return jax.nn.sigmoid(x)
def _layernorm(x, axis=-1, eps=1e-5):
    m = jnp.mean(x, axis=axis, keepdims=True)
    v = jnp.var(x, axis=axis, keepdims=True)
    return (x - m) / jnp.sqrt(v + eps)
def _scatter_add(tgt, idx, src, axis=0):
    return tgt.at[idx].add(src)
def _segment_sum(src, seg, n):
    return jax.ops.segment_sum(src, seg, n)

kernel_name = 'mk_adj_resnorm_d2_adj_256_9dc9c4'

def setup_inputs(seed: int = 0):
    np.random.seed(seed)
    _w = jnp.asarray
    def _rec_inputs():
        import jax
        import jax.numpy as jnp
        _gk = jax.random.key(seed)
        x = -0.0005207 + 1.001 * jax.random.normal(jax.random.fold_in(_gk, 1), (8, 2048, 256), jnp.float32)
        _a = jax.random.bernoulli(jax.random.fold_in(_gk, 2), 0.00390625, (2048, 2048))
        _a = jnp.logical_or(_a, jnp.swapaxes(_a, -1, -2))
        _a = jnp.logical_or(_a, jnp.eye(2048, dtype=bool))
        adj = _a.astype(jnp.int32)
        return x, adj
    x, adj = _rec_inputs()
    def _L0_gnn_setup():
        import jax, jax.numpy as jnp
        import numpy as np
        import math
        CHUNK = 256
        NUM_HEADS = 4
        EPS = 1e-05
        key = jax.random.key(seed)
        ks = jax.random.split(key, 12)
        B, N, F = (4, 2048, 256)
        x = jax.random.normal(ks[0], (B, N, F), dtype=jnp.float32)
        adj_matrix = jax.random.randint(ks[1], (N, N), 0, 2, dtype=jnp.int32)
        s = 1.0 / math.sqrt(F)
        Wq = jax.random.normal(ks[2], (F, F), dtype=jnp.float32) * s
        bq = jnp.zeros((F,), dtype=jnp.float32)
        Wk = jax.random.normal(ks[3], (F, F), dtype=jnp.float32) * s
        bk = jnp.zeros((F,), dtype=jnp.float32)
        Wv = jax.random.normal(ks[4], (F, F), dtype=jnp.float32) * s
        bv = jnp.zeros((F,), dtype=jnp.float32)
        Wo = jax.random.normal(ks[5], (F, F), dtype=jnp.float32) * s
        bo = jnp.zeros((F,), dtype=jnp.float32)
        gamma = jnp.ones((F,), dtype=jnp.float32)
        beta = jnp.zeros((F,), dtype=jnp.float32)
        return {'x': x, 'adj_matrix': adj_matrix, 'Wq': Wq, 'bq': bq, 'Wk': Wk, 'bk': bk, 'Wv': Wv, 'bv': bv, 'Wo': Wo, 'bo': bo, 'gamma': gamma, 'beta': beta}
    _L0_gnn_all = _L0_gnn_setup()
    _L0_gnn_in = {k: v for k, v in _L0_gnn_all.items() if k in ('Wq', 'bq', 'Wk', 'bk', 'Wv', 'bv', 'Wo', 'bo', 'gamma', 'beta', )}
    del _L0_gnn_all

    def _L1_gnn_setup():
        import jax, jax.numpy as jnp
        import numpy as np
        B, N, F_IN, F_OUT = (8, 2048, 256, 256)
        key = jax.random.key(seed)
        k1, k2, k3, k4 = jax.random.split(key, 4)
        x = jax.random.normal(k1, (B, N, F_IN), dtype=jnp.float32)
        W = jax.random.normal(k2, (F_IN, F_OUT), dtype=jnp.float32) * (1.0 / np.sqrt(F_IN))
        a = jax.random.normal(k3, (2 * F_OUT, 1), dtype=jnp.float32) * (1.0 / np.sqrt(2 * F_OUT))
        adj = jax.random.randint(k4, (N, N), 0, 2, dtype=jnp.int32)
        return {'x': x, 'W': W, 'a': a, 'adj': adj}
    _L1_gnn_all = _L1_gnn_setup()
    _L1_gnn_in = {k: v for k, v in _L1_gnn_all.items() if k in ('W', 'a', )}
    del _L1_gnn_all

    return {
        "x": x,
        "adj": adj,
        "L0_gnn_Wq": _L0_gnn_in["Wq"],
        "L0_gnn_bq": _L0_gnn_in["bq"],
        "L0_gnn_Wk": _L0_gnn_in["Wk"],
        "L0_gnn_bk": _L0_gnn_in["bk"],
        "L0_gnn_Wv": _L0_gnn_in["Wv"],
        "L0_gnn_bv": _L0_gnn_in["bv"],
        "L0_gnn_Wo": _L0_gnn_in["Wo"],
        "L0_gnn_bo": _L0_gnn_in["bo"],
        "L0_gnn_gamma": _L0_gnn_in["gamma"],
        "L0_gnn_beta": _L0_gnn_in["beta"],
        "L1_gnn_W": _L1_gnn_in["W"],
        "L1_gnn_a": _L1_gnn_in["a"],
    }

def reference(x, adj, L0_gnn_Wq, L0_gnn_bq, L0_gnn_Wk, L0_gnn_bk, L0_gnn_Wv, L0_gnn_bv, L0_gnn_Wo, L0_gnn_bo, L0_gnn_gamma, L0_gnn_beta, L1_gnn_W, L1_gnn_a):
    import jax
    import jax.numpy as jnp
    def _L0_gnn_ref(x, adj_matrix, Wq, bq, Wk, bk, Wv, bv, Wo, bo, gamma, beta):
        import jax, jax.numpy as jnp
        import numpy as np
        import math
        CHUNK = 256
        NUM_HEADS = 4
        EPS = 1e-05
        B, N, Fin = x.shape
        H = NUM_HEADS
        Dout = Wq.shape[0]
        Dh = Dout // H
        Nc = N // CHUNK
        q = (x @ Wq.T + bq).reshape(B, N, H, Dh).transpose(0, 2, 1, 3)
        k = (x @ Wk.T + bk).reshape(B, N, H, Dh).transpose(0, 2, 1, 3)
        v = (x @ Wv.T + bv).reshape(B, N, H, Dh).transpose(0, 2, 1, 3)
        kc = k.reshape(B, H, Nc, CHUNK, Dh)
        vc = v.reshape(B, H, Nc, CHUNK, Dh)
        scores = jnp.einsum('bhnd,bhjcd->bhnjc', q, kc) / jnp.sqrt(jnp.asarray(Dh, dtype=q.dtype))
        scores = jnp.clip(scores, -10.0, 10.0)
        mask = adj_matrix.reshape(N, Nc, CHUNK)[None, None]
        scores = jnp.where(mask == 0, jnp.asarray(-10.0, scores.dtype), scores)
        attn = jax.nn.softmax(scores, axis=-1)
        ctx = jnp.einsum('bhnjc,bhjcd->bhnd', attn, vc)
        ctx = ctx.transpose(0, 2, 1, 3).reshape(B, N, Dout)
        out = ctx @ Wo.T + bo
        out = out + x
        mu = jnp.mean(out, axis=-1, keepdims=True)
        var = jnp.mean(jnp.square(out - mu), axis=-1, keepdims=True)
        out = (out - mu) * jax.lax.rsqrt(var + EPS) * gamma + beta
        return out

    def _L1_gnn_ref(x, W, a, adj):
        import jax, jax.numpy as jnp
        import numpy as np
        B, N, F_IN, F_OUT = (8, 2048, 256, 256)
        h = jnp.einsum('bnf,fo->bno', x, W)
        F = W.shape[1]
        a1 = a[:F, 0]
        a2 = a[F:, 0]
        s1 = jnp.einsum('bno,o->bn', h, a1)
        s2 = jnp.einsum('bno,o->bn', h, a2)
        e = jax.nn.leaky_relu(s1[:, :, None] + s2[:, None, :], negative_slope=0.2)
        mask = adj.astype(h.dtype)[None, :, :]
        e = e + (1.0 - mask) * -1000000000.0
        attention = jax.nn.softmax(e, axis=-1)
        out = jnp.einsum('bnm,bmo->bno', attention, h)
        return out

    x = _layernorm(x + _L0_gnn_ref(x, adj, L0_gnn_Wq, L0_gnn_bq, L0_gnn_Wk, L0_gnn_bk, L0_gnn_Wv, L0_gnn_bv, L0_gnn_Wo, L0_gnn_bo, L0_gnn_gamma, L0_gnn_beta), axis=-1)
    x = _layernorm(x + _L1_gnn_ref(x, L1_gnn_W, L1_gnn_a, adj), axis=-1)
    return x


_drawn_inputs = setup_inputs


def setup_inputs(seed=0):
    import zlib

    import numpy as np

    out = dict(_drawn_inputs(seed))
    spreads = {'L0_gnn_bq': (0.0, 0.354),
     'L0_gnn_bk': (0.0, 2.0),
     'L0_gnn_bv': (0.0, 0.1),
     'L0_gnn_bo': (0.0, 0.1),
     'L0_gnn_gamma': (1.0, 0.2),
     'L0_gnn_beta': (0.0, 0.1)}
    factors = {}
    for name, (base, spread) in spreads.items():
        noise = np.random.default_rng([zlib.crc32(name.encode()), seed]).standard_normal(out[name].shape)
        drawn = base * np.exp(spread * noise) if base else spread * noise
        out[name] = jnp.asarray(drawn.astype(out[name].dtype))
    for name, factor in factors.items():
        out[name] = (out[name] * factor).astype(out[name].dtype)
    return out
```

```python
from contextlib import ExitStack

import numpy as np
import concourse.bass as bass
from concourse import mybir

ALU = mybir.AluOpType
ACT = mybir.ActivationFunctionType
AX = mybir.AxisListType
F32 = mybir.dt.float32
F16 = mybir.dt.float16
BF16 = mybir.dt.bfloat16
I32 = mybir.dt.int32
RMAX = bass.bass_isa.ReduceOp.max

P = 128
WS = 64.0
EPS = 1e-5


def adj_resnorm_kernel(nc, x, adj, Wq, bq, Wk, bk, Wv, bv, Wo, bo, gamma, beta, W1, a1, out):
    B, N, F = x.shape
    H = 4
    DH = F // H
    FT = F // P
    MT = N // P
    BLK = 512
    NB = N // BLK
    NT = BLK // P
    CHUNK = 256
    KT = CHUNK // P
    CH = N // CHUNK
    STEPS = H * CH
    TB = NB * STEPS
    DV = DH + 1
    SC = float(np.sqrt(DH)) * WS * WS
    CLIP = 10.0 * SC
    GS = 2.0 ** -11
    SLOPE = 0.2
    assert N == MT * P and F == 256 and CLIP == 10.0 * 2 ** 15 and FT == 2

    with ExitStack() as ctx:
        def sb(name, shape, dt):
            return ctx.enter_context(nc.sbuf_tensor(name, shape, dt))

        def sem(name):
            return ctx.enter_context(nc.semaphore(name))

        limit = sb("limit", [P, MT, N], BF16)
        Q = sb("Q", [P, NB, H, BLK], F16)
        K1 = sb("K1", [P, H, N], F16)
        K2 = sb("K2", [P, H, N], F16)
        V = sb("V", [P, MT, H * DV], F32)
        probs = sb("probs", [P, 4, KT, BLK], F32)
        xTh = sb("xTh", [P, FT, N], F16)
        xTl = sb("xTl", [P, FT, N], F16)
        xin = sb("xin", [P, NT, F], F32)
        xres = sb("xres", [P, NT, F], F32)
        r1 = sb("r1", [P, NT, F], F32)
        x1t = sb("x1t", [P, NT, F], F32)
        ctxs = sb("ctxs", [P, NT, F], F32)
        cTh = sb("cTh", [P, FT, BLK], F16)
        cTl = sb("cTl", [P, FT, BLK], F16)
        osb = sb("osb", [P, 4, NT, DV], F32)
        rz = sb("rz", [P, 4, NT], F32)
        scaled = sb("scaled", [P, NT, DH], F32)
        WTh = sb("WTh", [P, 4, FT, F], F16)
        WTl = sb("WTl", [P, 4, FT, F], F16)
        W1h = sb("W1h", [P, FT, F + 2], F16)
        W1l = sb("W1l", [P, FT, F + 2], F16)
        arh = sb("arh", [P, FT, P], F16)
        arl = sb("arl", [P, FT, P], F16)
        rows = sb("rows", [P, 4, F], F32)
        bqk = sb("bqk", [P, 2, FT], F32)
        ident = sb("ident", [P, P], F32)
        identb = sb("identb", [P, P], BF16)
        ones = sb("ones", [P, P], F32)
        s12 = sb("s12", [P, MT, 2], F32)
        s2m = sb("s2m", [P, 2], F32)
        st = sb("st", [P, NT, 6], F32)
        mv = sb("mv", [P, NT, 2], F32)
        rs = sb("rs", [P, 2, NT], F32)
        mhalf = sb("mhalf", [P, NT], F32)
        msm = sb("msm", [P, 6, NT], F32)
        lrz = sb("lrz", [P, NT], F32)
        x1s = Q[:, :, :, :].rearrange("p a b c -> p (a b c)").bitcast(F32).rearrange(
            "p (b t f) -> p b t f", b=NB, t=NT)
        k1f = K1[:, :, :].rearrange("p a b -> p (a b)").bitcast(F32)
        k2f = K2[:, :, :].rearrange("p a b -> p (a b)").bitcast(F32)
        s1b = k1f[:, 0:N]
        mb = k1f[:, N:2 * N]
        run = k2f[:, 0:BLK]
        diag = k2f[:, BLK:2 * BLK].rearrange("p (t c) -> p t c", t=NT)
        adji = K1[:, :, :].rearrange("p a b -> p (a b)").bitcast(I32).rearrange("p (s n) -> p s n", s=2)
        adjb = K2[:, :, :].rearrange("p a b -> p (a b)").bitcast(BF16)[:, 0:2 * N].rearrange("p (s n) -> p s n", s=2)
        wst = Q[:, :, :, :].rearrange("p a b c -> p (a b c)").bitcast(F32)
        wnat = wst[:, 0:4 * FT * F].rearrange("p (w t f) -> p w t f", w=4, t=FT)
        w1f = wst[:, 2048:2048 + FT * (F + 2)].rearrange("p (t f) -> p t f", t=FT)
        abc = wst[:, 2600:2600 + 2 * F].rearrange("p (a f) -> p a f", a=2)
        wtmp = probs[:, 0, :, :].rearrange("p a c -> p (a c)").rearrange("p (a t f) -> p a t f", a=2, t=FT)

        S = ctx.enter_context(nc.psum_tensor("S", [P, 2, KT, BLK], F32))
        O = ctx.enter_context(nc.psum_tensor("O", [P, 2, BLK], F32))
        C = ctx.enter_context(nc.psum_tensor("C", [P, 2, BLK], F32))
        Sf = S[:, :, :, :].rearrange("p a b c -> p (a b) c")
        Sb = S[:, :, :, :].rearrange("p a b c -> p a (b c)").bitcast(BF16)
        Cn = C[:, :, :].rearrange("p a c -> p (a c)").rearrange("p (t f) -> p t f", t=NT)

        w_in, row_in, const_made = sem("w_in"), sem("row_in"), sem("const_made")
        wT_psum, wT_hi, wT_split = sem("wT_psum"), sem("wT_hi"), sem("wT_split")
        wa_made, w1_hi, w1_split, bias_made = sem("wa_made"), sem("w1_hi"), sem("w1_split"), sem("bias_made")
        adj_in = [sem("adj_in0"), sem("adj_in1")]
        adj_bf, adj_T, lim_act, lim_dve = sem("adj_bf"), sem("adj_T"), sem("lim_act"), sem("lim_dve")
        x_in, xT_psum, xT_hi, xT_split = sem("x_in"), sem("xT_psum"), sem("xT_hi"), sem("xT_split")
        q_psum, k_psum, v_psum = sem("q_psum"), sem("k_psum"), sem("v_psum")
        q_hi, k_hi, q_split, k_split = sem("q_hi"), sem("k_hi"), sem("q_split"), sem("k_split")
        k_swapped, v_made, v_ones = sem("k_swapped"), sem("v_made"), sem("v_ones")
        scored, clipped, exped, pv_done = sem("scored"), sem("clipped"), sem("exped"), sem("pv_done")
        o_read, rz_made, mult_done, summed = sem("o_read"), sem("rz_made"), sem("mult_done"), sem("summed")
        cT_psum, cT_hi, cT_split = sem("cT_psum"), sem("cT_hi"), sem("cT_split")
        res_in, res_bo, res_made = sem("res_in"), sem("res_bo"), sem("res_made")
        mix_psum, mix_read = sem("mix_psum"), sem("mix_read")
        ln_stats = [sem(f"ln{i}_stats") for i in range(3)]
        ln_mean = [sem(f"ln{i}_mean") for i in range(3)]
        ln_eps = [sem(f"ln{i}_eps") for i in range(3)]
        ln_rstd = [sem(f"ln{i}_rstd") for i in range(3)]
        ln_done = [sem(f"ln{i}_done") for i in range(3)]
        y_mult, y_made = sem("y_mult"), sem("y_made")
        x1_saved, x1T_psum, x1T_hi, x1T_split = sem("x1_saved"), sem("x1T_psum"), sem("x1T_hi"), sem("x1T_split")
        h_psum, h_read, h_ones = sem("h_psum"), sem("h_read"), sem("h_ones")
        s1b_psum, s1b_made, s12_made = sem("s1b_psum"), sem("s1b_made"), sem("s12_made")
        s2m_part, s2m_made = sem("s2m_part"), sem("s2m_made")
        run_step, run_T, max_step = sem("run_step"), sem("run_T"), sem("max_step")
        lmax, diag_made = sem("lmax"), sem("diag_made")
        mb_psum, mb_made = sem("mb_psum"), sem("mb_made")
        g_summed, g_leaky, g_masked, g_shifted, g_exped = sem("g_summed"), sem("g_leaky"), sem("g_masked"), sem("g_shifted"), sem("g_exped")
        g_used, acc_done, lrz_made, acc_read = sem("g_used"), sem("acc_done"), sem("lrz_made"), sem("acc_read")
        stored = sem("stored")
        waits_over = sem("waits_over")

        AHEAD = 1
        from_ahead = (xT_psum, y_made, summed, cT_psum, x1T_psum, x1_saved, acc_done, stored, mix_psum, adj_T, run_T,
                      lim_act, lim_dve, s1b_made, q_split, k_split, v_made, x1T_split, h_read, mb_made, acc_read)

        block = ctx.enter_context(nc.Block())
        MAXSTEPS = 6
        RUN_AT = [3, 3, 3, 3, 2, 2]

        def blk(n):
            return bass.ts(n, BLK)

        def apart(eng):
            eng.sem_inc(waits_over, 1)

        @block.sync
        def _(sp):
            for i, w in enumerate((Wq, Wk, Wv, Wo)):
                sp.dma_start(wnat[:, i, :, :], w.rearrange("(t p) f -> p t f", p=P)).then_inc(w_in, 16)
            sp.dma_start(w1f[:, :, 0:F], W1.rearrange("(t p) f -> p t f", p=P)).then_inc(w_in, 16)
            for i, r in enumerate((bv, bo, gamma, beta)):
                sp.dma_start(rows[:, i, :], r.rearrange("(a f) -> a f", a=1).to_broadcast([P, F])).then_inc(row_in, 16)
            for i in range(2):
                sp.dma_start(abc[:, i, :], a1[i * F:(i + 1) * F, :].rearrange("f a -> a f").to_broadcast([P, F])).then_inc(row_in, 16)
            for i, r in enumerate((bq, bk)):
                sp.dma_start(bqk[:, i, :], r.rearrange("(t p) -> p t", p=P), allow_slow_non_contiguous=True).then_inc(row_in, 16)
            adj_v = adj.rearrange("(t p) m -> t p m", p=P)
            for s in range(2):
                sp.dma_start(adji[:, s, :], adj_v[s]).then_inc(adj_in[s], 16)
            with sp.Fori(1, MT // 2) as i:
                for s in range(2):
                    sp.wait_ge(adj_bf, i * 2 + s - 1)
                    sp.dma_start(adji[:, s, :], adj_v[i * 2 + s]).then_inc(adj_in[s], 16)

            x_v = x.rearrange("b (k t p) f -> (b k) p t f", t=NT, p=P)
            out_v = out.rearrange("b (k t p) f -> (b k) p t f", t=NT, p=P)
            halves = (slice(0, 64), slice(64, 128))

            def load_x(b, n, first=False):
                if not first:
                    sp.wait_ge(xT_psum, b * NB + n + AHEAD)
                sp.dma_start(xin[:, :, :], x_v[b * NB + n]).then_inc(x_in, 16)

            def swap_k(b, n):
                sp.wait_ge(k_split, b * NB + n + 1 + AHEAD)
                for i in range(2):
                    sp.dma_start(K2[halves[i], :, blk(n)], K1[halves[1 - i], :, blk(n)]).then_inc(k_swapped, 16)

            with sp.Fori(0, B) as b:
                sp.wait_ge(xT_psum, b * NB + AHEAD)
                load_x(b, 0, first=True)
                load_x(b, 1)
                with sp.Fori(0, NB - 2) as n:
                    load_x(b, n + 2)
                    swap_k(b, n)
                with sp.Fori(NB - 2, NB) as n:
                    swap_k(b, n)
                with sp.Fori(0, NB) as n:
                    sp.wait_ge(y_made, b * NB + n + AHEAD)
                    sp.dma_start(xres[:, :, :], x_v[b * NB + n]).then_inc(res_in, 16)
                    sp.wait_ge(ln_done[1], b * NB + n + 1)
                    sp.dma_start(x1s[:, n, :, :], x1t[:, :, :]).then_inc(x1_saved, 16)
                with sp.Fori(0, NB) as n:
                    sp.wait_ge(ln_done[2], b * NB + n + 1)
                    sp.dma_start(out_v[b * NB + n], x1t[:, :, :]).then_inc(stored, 16)
            sp.wait_ge(stored, B * NB * 16 + AHEAD)

        @block.gpsimd
        def _(pool):
            for s in from_ahead:
                pool.sem_inc(s, AHEAD)
            pool.memset(ident[:, :], 0.0).then_inc(const_made, 1)
            pool.memset(identb[:, :], 0.0).then_inc(const_made, 1)
            pool.memset(ones[:, :], 1.0).then_inc(const_made, 1)
            pool.memset(mhalf[:, :], -0.5).then_inc(const_made, 1)
            pool.wait_ge(const_made, 4)
            for m in (ident, identb):
                pool.affine_select(out=m[:, :], in_=m[:, :], compare_op=ALU.not_equal, fill=1.0,
                                   base=0, pattern=[[-1, P]], channel_multiplier=1).then_inc(const_made, 1)

            def rstd(kind, g):
                pool.wait_ge(ln_mean[kind], g + 1)
                apart(pool)
                pool.tensor_scalar(rs[:, 0, :], mv[:, :, 1], EPS, None, ALU.add).then_inc(ln_eps[kind], 1)
                pool.wait_ge(ln_eps[kind], g + 1)
                pool.tensor_tensor(rs[:, 1, :], rs[:, 0, :], mhalf[:, :], ALU.pow).then_inc(ln_rstd[kind], 1)

            def accumulate(b, n, s, head=False):
                t = b * TB + n * STEPS + s
                h, j, slot = s // CH, s % CH, s % 4
                dst = ctxs[:, :, h * DH:(h + 1) * DH]
                first = j == 0
                pool.wait_ge(summed, t + AHEAD)
                pool.wait_ge(rz_made, t + 1)
                if first and h == 0 and not head:
                    pool.wait_ge(cT_psum, (b * NB + n) * 2 - 1 + AHEAD)
                if first and h == 2:
                    pool.wait_ge(cT_psum, (b * NB + n) * 2 + AHEAD)
                o = pool.tensor_tensor(dst if first else scaled[:, :, :], osb[:, slot, :, 0:DH],
                                       rz[:, slot, :].unsqueeze(2).to_broadcast([P, NT, DH]), ALU.mult)
                if first:
                    o.then_inc(summed, 1)
                else:
                    o.then_inc(mult_done, 1)
                    pool.wait_ge(mult_done, (b * NB + n) * (STEPS - H) + s - h)
                    pool.tensor_tensor(dst, dst, scaled[:, :, :], ALU.add).then_inc(summed, 1)

            def bcast(i):
                return rows[:, i, :].unsqueeze(1).to_broadcast([P, NT, F])

            def mix_residuals(g):
                pool.wait_ge(res_in, (g + 1) * 16)
                pool.wait_ge(x1T_psum, g + AHEAD)
                pool.wait_ge(x1_saved, g * 16 + AHEAD)
                pool.tensor_tensor(x1t[:, :, :], xres[:, :, :], bcast(1), ALU.add).then_inc(res_bo, 1)
                pool.tensor_tensor(xres[:, :, :], xres[:, :, :], bcast(3), ALU.add).then_inc(res_made, 1)

            def mix_y(g):
                pool.wait_ge(ln_done[0], g + 1)
                pool.tensor_tensor(r1[:, :, :], r1[:, :, :], bcast(2), ALU.mult).then_inc(y_mult, 1)
                pool.wait_ge(y_mult, g + 1)
                pool.wait_ge(res_made, g + 1)
                pool.tensor_tensor(r1[:, :, :], r1[:, :, :], xres[:, :, :], ALU.add).then_inc(y_made, 1)

            pool_mix = {10: mix_residuals, 14: lambda g: rstd(0, g), 16: mix_y, 20: lambda g: rstd(1, g)}

            def attend(b, n, first):
                for s in range(STEPS):
                    if s >= 3:
                        accumulate(b, n, s - 3, head=first)
                    elif not first:
                        accumulate(b, n - 1, STEPS + s - 3)
                    if not first and s in pool_mix:
                        pool_mix[s](b * NB + n - 1)

            def shift(b, n, j):
                k = b * NB * CH + n * CH + j
                pool.wait_ge(g_masked, k + 1)
                apart(pool)
                pool.tensor_tensor(probs[:, j % 4, :, :], probs[:, j % 4, :, :],
                                   mb[:, blk(n)].unsqueeze(1).to_broadcast([P, KT, BLK]),
                                   ALU.subtract).then_inc(g_shifted, 1)

            pool.wait_ge(row_in, 8 * 16)
            with pool.Fori(0, B) as b:
                pool.wait_ge(acc_done, b * NB * NT + AHEAD)
                vo = V[:, :, :].rearrange("p m (h d) -> p m h d", h=H)[:, :, :, DH]
                apart(pool)
                pool.memset(vo, 1.0).then_inc(v_ones, 1)
                pool.wait_ge(stored, b * NB * 16 + AHEAD)
                attend(b, 0, True)
                with pool.Fori(1, NB) as n:
                    attend(b, n, False)
                for s in range(3):
                    accumulate(b, NB - 1, STEPS + s - 3)
                for s in sorted(pool_mix):
                    pool_mix[s](b * NB + NB - 1)
                pool.wait_ge(pv_done, (b + 1) * TB)
                apart(pool)
                pool.memset(V[:, :, 0:1], 1.0).then_inc(h_ones, 1)
                pool.wait_ge(s2m_part, b + 1)
                apart(pool)
                pool.partition_all_reduce(s2m[:, 1:2], s2m[:, 0:1], P, RMAX).then_inc(s2m_made, 1)

                def gat(n, first):
                    pool.wait_ge(mb_made, b * NB + n + 1 + AHEAD)
                    for j in range(CH):
                        shift(b, n, j)
                        if j == 3 and not first:
                            rstd(2, b * NB + n - 1)
                gat(0, True)
                with pool.Fori(1, NB) as n:
                    gat(n, False)
                rstd(2, b * NB + NB - 1)

        @block.scalar
        def _(act):
            for i in range(4):
                act.wait_ge(wT_psum, i + 1)
                act.activation(WTh[:, i, :, :], Sf[:, i, :].rearrange("p (t f) -> p t f", t=FT), ACT.Copy, scale=WS).then_inc(wT_hi, 1)
            act.wait_ge(wa_made, 1)
            act.activation(W1h[:, :, :], w1f, ACT.Copy, scale=WS).then_inc(w1_hi, 1)
            act.activation(arh[:, :, :], w1f[:, :, F:F + 1].to_broadcast([P, FT, P]), ACT.Copy, scale=WS).then_inc(w1_hi, 1)
            with act.Fori(0, MT // 2) as i:
                act.wait_ge(adj_T, i * 2 + 1 + AHEAD)
                apart(act)
                act.activation(limit[:, :, bass.ds(i * (2 * P), P)], Sb[:, 0, :].rearrange("p (m c) -> p m c", m=MT),
                               ACT.Copy).then_inc(lim_act, 1)

            def split_hi(b, n):
                g = b * NB + n
                act.wait_ge(q_psum, g + 1)
                apart(act)
                for o in range(FT):
                    for r in range(2):
                        rr = slice(64 * r, 64 * r + 64)
                        last = act.activation(Q[rr, n, 2 * o + r, :], Sf[rr, o, :], ACT.Identity, bias=bqk[rr, 0, o:o + 1])
                last.then_inc(q_hi, 1)
                act.wait_ge(k_psum, g + 1)
                apart(act)
                for o in range(FT):
                    for r in range(2):
                        rr = slice(64 * r, 64 * r + 64)
                        last = act.activation(K1[rr, 2 * o + r, blk(n)], Sf[rr, 2 + o, :], ACT.Identity, bias=bqk[rr, 1, o:o + 1])
                last.then_inc(k_hi, 1)

            def xT_value(b, n):
                act.wait_ge(xT_psum, b * NB + n + 1 + AHEAD)
                apart(act)
                act.activation(xTh[:, :, blk(n)], C[:, :, :], ACT.Copy).then_inc(xT_hi, 1)

            def exps(b, n, s):
                t = b * TB + n * STEPS + s
                act.wait_ge(clipped, t + 1)
                act.activation(probs[:, s % 4, :, :], probs[:, s % 4, :, :], ACT.Exp, scale=1.0 / SC).then_inc(exped, 1)

            def read_o(b, n, s, early=False):
                t = b * TB + n * STEPS + s
                act.wait_ge(pv_done, t + 1)
                if not early:
                    act.wait_ge(summed, t - 3 + AHEAD)
                act.activation(osb[:, s % 4, :, :], O[:, s % 2, 0:NT * DV].rearrange("p (t d) -> p t d", t=NT), ACT.Copy).then_inc(o_read, 1)

            def mix_value(g, o):
                act.wait_ge(cT_psum, g * 2 + o + 1 + AHEAD)
                act.wait_ge(mix_psum, g + AHEAD)
                act.activation(cTh[:, o, :], C[:, o, :], ACT.Copy).then_inc(cT_hi, 1)

            def x1T_value(b, n):
                act.wait_ge(x1T_psum, b * NB + n + 1 + AHEAD)
                apart(act)
                act.activation(xTh[:, :, blk(n)], C[:, :, :], ACT.Copy).then_inc(x1T_hi, 1)

            def attend(b, n, first):
                for s in range(STEPS):
                    exps(b, n, s)
                    if s >= 2:
                        read_o(b, n, s - 2, early=first and s < 6)
                    elif not first:
                        read_o(b, n - 1, STEPS + s - 2)
                    if s == 8 and not first:
                        mix_value(b * NB + n - 1, 1)
                    if s == 22 and not first:
                        x1T_value(b, n - 1)
                    if s == 28:
                        mix_value(b * NB + n, 0)

            def pair_sum(b, n, j, early):
                if not early:
                    if j < 3:
                        act.wait_ge(g_used, (b * NB + n - 1) * (CH - 1) + j + 5)
                    elif j == 3:
                        act.wait_ge(acc_done, (b * NB + n) * NT + AHEAD)
                    else:
                        act.wait_ge(g_used, (b * NB + n) * (CH - 1) + j - 3)
                elif j > 3:
                    act.wait_ge(g_used, (b * NB + n) * (CH - 1) + j - 3)
                apart(act)
                for i in range(KT):
                    m = j * KT + i
                    last = act.activation(probs[:, j % 4, i, :], s1b[:, blk(n)], ACT.Identity, bias=s12[:, m, 1:2])
                last.then_inc(g_summed, 1)

            def read_mb(b, n):
                act.wait_ge(mb_psum, b * NB + n + 1)
                apart(act)
                act.activation(mb[:, blk(n)], O[:, 1, :], ACT.Copy).then_inc(mb_made, 1)

            def gat(b, n, first, last):
                for j in range(CH):
                    if j + 2 < CH:
                        pair_sum(b, n, j + 2, first)
                    elif not last:
                        pair_sum(b, n + 1, j + 2 - CH, False)
                    if j == CH - 1 and not last:
                        read_mb(b, n + 1)
                    k = (b * NB + n) * CH + j
                    act.wait_ge(g_shifted, k + 1)
                    act.activation(probs[:, j % 4, :, :], probs[:, j % 4, :, :], ACT.Exp, scale=1.0 / GS).then_inc(g_exped, 1)

            act.wait_ge(bias_made, 1)
            with act.Fori(0, B) as b:
                xT_value(b, 0)
                with act.Fori(0, NB - 1) as n:
                    xT_value(b, n + 1)
                    split_hi(b, n)
                split_hi(b, NB - 1)
                attend(b, 0, True)
                with act.Fori(1, NB) as n:
                    attend(b, n, False)
                for s in range(2):
                    read_o(b, NB - 1, STEPS + s - 2)
                mix_value(b * NB + NB - 1, 1)
                x1T_value(b, NB - 1)
                with act.Fori(0, NB) as n:
                    for i in range(NT):
                        act.wait_ge(h_psum, (b * NB + n) * NT + i + 1)
                        apart(act)
                        act.activation(V[:, n * NT + i, 1:F + 3], Sf[:, i, 0:F + 2], ACT.Copy, scale=1.0 / WS).then_inc(h_read, 1)
                    act.wait_ge(s1b_psum, b * NB + n + 1)
                    apart(act)
                    act.activation(s1b[:, blk(n)], C[:, 0, :], ACT.Copy, scale=GS / WS).then_inc(s1b_made, 1)
                act.wait_ge(s1b_made, (b + 1) * NB + AHEAD)
                act.wait_ge(s12_made, b + 1)
                for j in range(2):
                    pair_sum(b, 0, j, True)
                read_mb(b, 0)
                gat(b, 0, True, False)
                with act.Fori(1, NB - 1) as n:
                    gat(b, n, False, False)
                gat(b, NB - 1, False, True)

        @block.vector
        def _(dve):
            for i in range(4):
                dve.wait_ge(wT_hi, i + 1)
                dve.scalar_tensor_tensor(WTl[:, i, :, :], Sf[:, i, :].rearrange("p (t f) -> p t f", t=FT), WS, WTh[:, i, :, :],
                                         ALU.mult, ALU.subtract).then_inc(wT_split, 1)
            dve.wait_ge(w_in, 5 * 16)
            dve.wait_ge(row_in, 8 * 16)
            for t in range(FT):
                for i in range(2):
                    last = dve.tensor_tensor(wtmp[:, i, t, :], w1f[:, t, 0:F], abc[:, i, :], ALU.mult)
            last.then_inc(run_step, 1)
            dve.wait_ge(run_step, 1)
            for i in range(2):
                last = dve.tensor_reduce(w1f[:, :, F + i], wtmp[:, i, :, :], AX.X, ALU.add)
            last.then_inc(wa_made, 1)
            dve.tensor_scalar(bqk[:, :, :], bqk[:, :, :], WS, None, ALU.mult).then_inc(bias_made, 1)
            dve.wait_ge(w1_hi, 2)
            dve.scalar_tensor_tensor(W1l[:, :, :], w1f, WS, W1h[:, :, :], ALU.mult, ALU.subtract).then_inc(w1_split, 1)
            dve.scalar_tensor_tensor(arl[:, :, :], w1f[:, :, F:F + 1].to_broadcast([P, FT, P]), WS, arh[:, :, :],
                                     ALU.mult, ALU.subtract).then_inc(w1_split, 1)

            def to_limit(i, s):
                dve.wait_ge(adj_in[s], i * 16 + 16)
                dve.wait_ge(adj_T, i * 2 + AHEAD)
                dve.tensor_scalar(adjb[:, s, :], adji[:, s, :], 2 * CLIP, -CLIP, ALU.mult, ALU.add).then_inc(adj_bf, 1)

            with dve.Fori(0, MT // 2) as i:
                to_limit(i, 0)
                to_limit(i, 1)
                dve.wait_ge(adj_T, i * 2 + 2 + AHEAD)
                dve.tensor_copy(limit[:, :, bass.ds(i * (2 * P) + P, P)], Sb[:, 1, :].rearrange("p (m c) -> p m c", m=MT)).then_inc(lim_dve, 1)

            def xT_rest(b, n):
                dve.wait_ge(xT_hi, b * NB + n + 1)
                dve.tensor_tensor(xTl[:, :, blk(n)], C[:, :, :], xTh[:, :, blk(n)], ALU.subtract).then_inc(xT_split, 1)

            def split_rest(b, n):
                g = b * NB + n
                for w, ready, done in ((0, q_hi, q_split), (1, k_hi, k_split)):
                    dve.wait_ge(ready, g + 1)
                    for o in range(FT):
                        for r in range(2):
                            rr = slice(64 * r, 64 * r + 64)
                            ll = slice(64 - 64 * r, 128 - 64 * r)
                            val = (lambda s: Q[s, n, 2 * o + r, :] if w == 0 else K1[s, 2 * o + r, blk(n)])
                            last = dve.scalar_tensor_tensor(val(ll), Sf[rr, 2 * w + o, :], bqk[rr, w, o:o + 1], val(rr),
                                                            ALU.add, ALU.subtract)
                    last.then_inc(done, 1)
                dve.wait_ge(v_psum, g + 1)
                for t in range(NT):
                    last = dve.scalar_tensor_tensor(
                        V[:, n * NT + t, :].rearrange("p (h d) -> p h d", h=H)[:, :, 0:DH],
                        O[:, t // 2, (t % 2) * F:(t % 2 + 1) * F].rearrange("p (h d) -> p h d", h=H), 1.0 / WS,
                        rows[:, 0, :].rearrange("p (h d) -> p h d", h=H), ALU.mult, ALU.add)
                last.then_inc(v_made, 1)

            def clip(b, n, s):
                t = b * TB + n * STEPS + s
                j = s % CH
                dve.wait_ge(scored, t + 1)
                dve.scalar_tensor_tensor(probs[:, s % 4, :, :], S[:, s % 2, :, :], -CLIP,
                                         limit[:, j * KT:(j + 1) * KT, blk(n)], ALU.max, ALU.min).then_inc(clipped, 1)

            def recip(b, n, s):
                t = b * TB + n * STEPS + s
                dve.wait_ge(o_read, t + 1)
                dve.reciprocal(rz[:, s % 4, :], osb[:, s % 4, :, DH]).then_inc(rz_made, 1)

            def stats(kind, g):
                for t in range(NT):
                    last = dve.bn_stats(st[:, t, :], r1[:, t, :])
                last.then_inc(ln_stats[kind], 1)
                dve.wait_ge(ln_stats[kind], g + 1)
                apart(dve)
                for t in range(NT):
                    last = dve.bn_aggr(mv[:, t, :], st[:, t, :])
                last.then_inc(ln_mean[kind], 1)

            def normalise(kind, g, dst):
                dve.wait_ge(ln_rstd[kind], g + 1)
                for t in range(NT):
                    last = dve.tensor_scalar(dst[:, t, :], r1[:, t, :], mv[:, t, 0:1], rs[:, 1, t:t + 1], ALU.subtract, ALU.mult)
                last.then_inc(ln_done[kind], 1)

            def mix_rest(g, o):
                dve.wait_ge(cT_hi, g * 2 + o + 1)
                dve.tensor_tensor(cTl[:, o, :], C[:, o, :], cTh[:, o, :], ALU.subtract).then_inc(cT_split, 1)

            def mix_add(g):
                dve.wait_ge(mix_psum, g + 1 + AHEAD)
                dve.wait_ge(res_bo, g + 1)
                dve.scalar_tensor_tensor(r1[:, :, :], Cn, 1.0 / WS, x1t[:, :, :], ALU.mult, ALU.add).then_inc(mix_read, 1)
                dve.wait_ge(mix_read, g + 1)
                stats(0, g)

            def mix_stats2(g):
                dve.wait_ge(y_made, g + 1 + AHEAD)
                stats(1, g)

            dve_mix = {8: lambda g: mix_rest(g, 1), 12: mix_add, 15: lambda g: normalise(0, g, r1),
                       19: mix_stats2, 21: lambda g: normalise(1, g, x1t)}

            def x1T_rest(b, n):
                dve.wait_ge(x1T_hi, b * NB + n + 1)
                dve.tensor_tensor(xTl[:, :, blk(n)], C[:, :, :], xTh[:, :, blk(n)], ALU.subtract).then_inc(x1T_split, 1)

            def attend(b, n, first):
                for s in range(STEPS):
                    clip(b, n, s)
                    if s >= 3:
                        recip(b, n, s - 3)
                    elif not first:
                        recip(b, n - 1, STEPS + s - 3)
                    if not first and s in dve_mix:
                        dve_mix[s](b * NB + n - 1)
                    if not first and s == 23:
                        x1T_rest(b, n - 1)
                    if s == 29:
                        mix_rest(b * NB + n, 0)

            def run_max(b, n, m):
                c = (b * NB + n) * MT + m + 1
                if m == 0:
                    dve.wait_ge(run_T, b * NB + n + AHEAD)
                    dve.tensor_scalar(run, limit[:, m, blk(n)], s12[:, m, 1:2], None, ALU.min).then_inc(run_step, 1)
                else:
                    dve.wait_ge(run_step, c)
                    dve.scalar_tensor_tensor(run, limit[:, m, blk(n)], s12[:, m, 1:2], run, ALU.min, ALU.max).then_inc(run_step, 1)

            def row_max(b, n):
                g = b * NB + n
                G, some, cand, sel, lk, M = (msm[:, i, :] for i in range(6))
                steps = [0]

                def link(o):
                    steps[0] += 1
                    o.then_inc(max_step, 1)
                    dve.wait_ge(max_step, g * MAXSTEPS + steps[0])

                dve.wait_ge(run_T, g + 1 + AHEAD)
                link(dve.tensor_reduce(G, O[:, 0, :].rearrange("p (t c) -> p t c", t=NT), AX.X, ALU.max))
                link(dve.tensor_scalar(some, G, -CLIP, None, ALU.is_gt))
                link(dve.scalar_tensor_tensor(cand, some, -2.0 ** 60, s2m[:, 1:2].to_broadcast([P, NT]), ALU.mult, ALU.add))
                link(dve.tensor_tensor(sel, G, cand, ALU.max))
                link(dve.tensor_tensor(lk, s12[:, bass.ts(n, NT), 0], sel, ALU.add))
                dve.tensor_scalar(some, some, CLIP, -CLIP, ALU.mult, ALU.add)
                link(dve.scalar_tensor_tensor(M, lk, SLOPE, lk, ALU.mult, ALU.max))
                dve.tensor_tensor(M, M, some, ALU.add).then_inc(lmax, 1)
                dve.wait_ge(lmax, g + 1)
                dve.tensor_tensor(diag, ident[:, :].unsqueeze(1).to_broadcast([P, NT, P]),
                                  M.unsqueeze(2).to_broadcast([P, NT, P]), ALU.mult).then_inc(diag_made, 1)

            def finish(b, n):
                g = b * NB + n
                for t in range(NT):
                    dve.wait_ge(acc_done, g * NT + t + 1 + AHEAD)
                    dve.reciprocal(lrz[:, t:t + 1], Sf[:, t, 0:1]).then_inc(lrz_made, 1)
                    dve.wait_ge(lrz_made, g * NT + t + 1)
                    dve.scalar_tensor_tensor(r1[:, t, :], Sf[:, t, 1:F + 1], lrz[:, t:t + 1], x1s[:, n, t, :],
                                             ALU.mult, ALU.add).then_inc(acc_read, 1)

            def finish_stats(g):
                dve.wait_ge(acc_read, (g + 1) * NT + AHEAD)
                stats(2, g)

            def finish_norm(g):
                dve.wait_ge(stored, g * 16 + AHEAD)
                normalise(2, g, x1t)

            def gat(b, n, first, last):
                m = 0
                for j in range(CH):
                    k = (b * NB + n) * CH + j
                    w = probs[:, j % 4, :, :]
                    dve.wait_ge(g_summed, k + 1)
                    dve.scalar_tensor_tensor(w, w, SLOPE, w, ALU.mult, ALU.max).then_inc(g_leaky, 1)
                    dve.wait_ge(g_leaky, k + 1)
                    dve.scalar_tensor_tensor(w, limit[:, j * KT:(j + 1) * KT, blk(n)], 0.0,
                                             w, ALU.min, ALU.add).then_inc(g_masked, 1)
                    if not first:
                        if j == 1:
                            finish(b, n - 1)
                        if j == 2:
                            finish_stats(b * NB + n - 1)
                        if j == 4:
                            finish_norm(b * NB + n - 1)
                    if not last:
                        if j < len(RUN_AT):
                            for _ in range(RUN_AT[j]):
                                run_max(b, n + 1, m)
                                m += 1
                        if j == 6:
                            row_max(b, n + 1)

            with dve.Fori(0, B) as b:
                xT_rest(b, 0)
                with dve.Fori(0, NB - 1) as n:
                    xT_rest(b, n + 1)
                    split_rest(b, n)
                split_rest(b, NB - 1)
                attend(b, 0, True)
                with dve.Fori(1, NB) as n:
                    attend(b, n, False)
                for s in range(3):
                    recip(b, NB - 1, STEPS + s - 3)
                for s in sorted(dve_mix):
                    dve_mix[s](b * NB + NB - 1)
                x1T_rest(b, NB - 1)
                dve.wait_ge(h_read, (b + 1) * MT + AHEAD)
                dve.tensor_scalar(s12[:, :, :], V[:, :, F + 1:F + 3], GS, None, ALU.mult).then_inc(s12_made, 1)
                dve.wait_ge(s12_made, b + 1)
                dve.tensor_reduce(s2m[:, 0:1], s12[:, :, 1], AX.X, ALU.max).then_inc(s2m_part, 1)
                for m in range(MT):
                    run_max(b, 0, m)
                dve.wait_ge(x1_saved, (b + 1) * NB * 16 + AHEAD)
                dve.wait_ge(s2m_made, b + 1)
                row_max(b, 0)
                gat(b, 0, True, False)
                with dve.Fori(1, NB - 1) as n:
                    gat(b, n, False, False)
                gat(b, NB - 1, False, True)
                finish(b, NB - 1)
                finish_stats(b * NB + NB - 1)
                finish_norm(b * NB + NB - 1)

        @block.tensor
        def _(pe):
            pe.wait_ge(const_made, 6)
            pe.wait_ge(w_in, 5 * 16)
            for i in range(4):
                for ft in range(FT):
                    for ot in range(FT):
                        last = pe.transpose(Sf[:, i, ft * F + ot * P:ft * F + (ot + 1) * P], wnat[:, i, ot, ft * P:(ft + 1) * P], ident[:, :])
                last.then_inc(wT_psum, 1)
            pe.wait_ge(wT_split, 4)
            with pe.Fori(0, MT // 2) as i:
                for s, lim in ((0, lim_act), (1, lim_dve)):
                    pe.wait_ge(adj_bf, i * 2 + s + 1)
                    pe.wait_ge(lim, i + AHEAD)
                    for m in range(MT):
                        last = pe.transpose(Sb[:, s, m * P:(m + 1) * P], adjb[:, s, m * P:(m + 1) * P], identb[:, :])
                    last.then_inc(adj_T, 1)

            def split_mm(dst, pairs):
                ops = [(lh, rh) for (lh, ll, rh, rl) in pairs] + [(lh, rl) for (lh, ll, rh, rl) in pairs] + \
                      [(ll, rh) for (lh, ll, rh, rl) in pairs]
                for i, (w, m) in enumerate(ops):
                    last = pe.matmul(dst, lhsT=w, rhs=m, start=i == 0, stop=i == len(ops) - 1)
                return last

            def xT(b, n, head):
                g = b * NB + n
                pe.wait_ge(x_in, g * 16 + 16)
                if head:
                    pe.wait_ge(s1b_made, b * NB + AHEAD)
                else:
                    pe.wait_ge(xT_split, g)
                for ft in range(FT):
                    for t in range(NT):
                        last = pe.transpose(C[:, ft, t * P:(t + 1) * P], xin[:, t, ft * P:(ft + 1) * P], ident[:, :])
                last.then_inc(xT_psum, 1)

            def qkv(b, n, head):
                g = b * NB + n
                pe.wait_ge(xT_split, g + 1)
                for w, psum, free in ((0, q_psum, q_split), (1, k_psum, k_split)):
                    pe.wait_ge(free, g + AHEAD)
                    for o in range(FT):
                        last = split_mm(Sf[:, 2 * w + o, :], [
                            (WTh[:, w, ft, o * P:(o + 1) * P], WTl[:, w, ft, o * P:(o + 1) * P],
                             xTh[:, ft, blk(n)], xTl[:, ft, blk(n)]) for ft in range(FT)])
                    last.then_inc(psum, 1)
                pe.wait_ge(v_made, g + AHEAD)
                for t in range(NT):
                    cols = bass.ds(n * BLK + t * P, P)
                    last = split_mm(O[:, t // 2, (t % 2) * F:(t % 2 + 1) * F], [
                        (xTh[:, ft, cols], xTl[:, ft, cols], WTh[:, 2, ft, :], WTl[:, 2, ft, :]) for ft in range(FT)])
                last.then_inc(v_psum, 1)

            def score(b, n, s, head=False):
                t = b * TB + n * STEPS + s
                h, j = s // CH, s % CH
                if not head:
                    pe.wait_ge(clipped, t - 1)
                for i in range(KT):
                    m = j * KT + i
                    for r, K in enumerate((K1, K2)):
                        last = pe.matmul(S[:, s % 2, i, :], lhsT=K[:, h, m * P:(m + 1) * P], rhs=Q[:, n, h, :],
                                         start=r == 0, stop=r == 1)
                last.then_inc(scored, 1)

            def pv(b, n, s, head=False):
                t = b * TB + n * STEPS + s
                h, j = s // CH, s % CH
                pe.wait_ge(exped, t + 1)
                if not head:
                    pe.wait_ge(o_read, t - 1)
                for q in range(NT):
                    for i in range(KT):
                        last = pe.matmul(O[:, s % 2, q * DV:(q + 1) * DV], lhsT=probs[:, s % 4, i, q * P:(q + 1) * P],
                                         rhs=V[:, j * KT + i, h * DV:(h + 1) * DV], start=i == 0, stop=i == KT - 1)
                last.then_inc(pv_done, 1)

            def mix_T(b, n, o):
                g = b * NB + n
                pe.wait_ge(summed, b * TB + n * STEPS + (o + 1) * STEPS // 2 + AHEAD)
                if o == 0:
                    pe.wait_ge(x1T_split, g + AHEAD)
                for t in range(NT):
                    last = pe.transpose(C[:, o, t * P:(t + 1) * P], ctxs[:, t, o * P:(o + 1) * P], ident[:, :])
                last.then_inc(cT_psum, 1)

            def mix_project(b, n):
                g = b * NB + n
                pe.wait_ge(cT_split, g * 2 + 2)
                for t in range(NT):
                    last = split_mm(Cn[:, t, :], [
                        (cTh[:, o, t * P:(t + 1) * P], cTl[:, o, t * P:(t + 1) * P], WTh[:, 3, o, :], WTl[:, 3, o, :])
                        for o in range(FT)])
                last.then_inc(mix_psum, 1)

            def x1T(b, n):
                pe.wait_ge(ln_done[1], b * NB + n + 1)
                for ft in range(FT):
                    for t in range(NT):
                        last = pe.transpose(C[:, ft, t * P:(t + 1) * P], x1t[:, t, ft * P:(ft + 1) * P], ident[:, :])
                last.then_inc(x1T_psum, 1)

            pe_mix = {6: lambda b, n: mix_T(b, n, 1), 10: mix_project, 22: x1T}

            def attend(b, n, first):
                for s in range(STEPS):
                    score(b, n, s, head=first and s < 2)
                    if s >= 2:
                        pv(b, n, s - 2, head=first and s < 4)
                    elif not first:
                        pv(b, n - 1, STEPS + s - 2)
                    if not first and s in pe_mix:
                        pe_mix[s](b, n - 1)
                    if s == 26:
                        mix_T(b, n, 0)

            def gat_sum(b, n, j, head):
                k = (b * NB + n) * CH + j
                pe.wait_ge(g_exped, k + 1)
                for q in range(NT):
                    if j == 0 and not head:
                        pe.wait_ge(acc_read, (b * NB + n - 1) * NT + q + 1 + AHEAD)
                    for i in range(KT):
                        last = pe.matmul(Sf[:, q, 0:F + 1], lhsT=probs[:, j % 4, i, q * P:(q + 1) * P],
                                         rhs=V[:, j * KT + i, 0:F + 1], start=j == 0 and i == 0,
                                         stop=j == CH - 1 and i == KT - 1)
                    if j == CH - 1:
                        last.then_inc(acc_done, 1)
                if j < CH - 1:
                    last.then_inc(g_used, 1)

            def run_transpose(b, n):
                pe.wait_ge(run_step, (b * NB + n) * MT + MT + 1)
                for t in range(NT):
                    last = pe.transpose(O[:, 0, t * P:(t + 1) * P], run[:, t * P:(t + 1) * P], ident[:, :])
                last.then_inc(run_T, 1)

            def spread_max(b, n):
                pe.wait_ge(diag_made, b * NB + n + 1)
                pe.wait_ge(mb_made, b * NB + n + AHEAD)
                pe.matmul(O[:, 1, :], lhsT=ones[:, :], rhs=k2f[:, BLK:2 * BLK], start=True, stop=True).then_inc(mb_psum, 1)

            def gat(b, n, first, last):
                for j in range(CH):
                    if not last and j == 6:
                        run_transpose(b, n + 1)
                    if not last and j == 7:
                        spread_max(b, n + 1)
                    gat_sum(b, n, j, first)

            pe.wait_ge(w1_split, 2)
            with pe.Fori(0, B) as b:
                pe.wait_ge(acc_read, b * MT + AHEAD)
                xT(b, 0, True)
                with pe.Fori(0, NB - 1) as n:
                    xT(b, n + 1, False)
                    qkv(b, n, False)
                qkv(b, NB - 1, False)
                pe.wait_ge(q_split, (b + 1) * NB + AHEAD)
                pe.wait_ge(k_swapped, (b + 1) * NB * 32)
                pe.wait_ge(v_made, (b + 1) * NB + AHEAD)
                pe.wait_ge(v_ones, b + 1)
                pe.wait_ge(lim_act, MT // 2 + AHEAD)
                pe.wait_ge(lim_dve, MT // 2 + AHEAD)
                attend(b, 0, True)
                with pe.Fori(1, NB) as n:
                    attend(b, n, False)
                for s in range(2):
                    pv(b, NB - 1, STEPS + s - 2)
                for s in sorted(pe_mix):
                    pe_mix[s](b, NB - 1)
                pe.wait_ge(x1T_split, (b + 1) * NB + AHEAD)
                apart(pe)
                with pe.Fori(0, NB) as n:
                    for t in range(NT):
                        g = (b * NB + n) * NT + t
                        pe.wait_ge(h_read, (b * NB + n) * NT + AHEAD)
                        cols = bass.ds(n * BLK + t * P, P)
                        split_mm(Sf[:, t, 0:F + 2], [
                            (xTh[:, ft, cols], xTl[:, ft, cols], W1h[:, ft, :], W1l[:, ft, :]) for ft in range(FT)]
                        ).then_inc(h_psum, 1)
                    pe.wait_ge(s1b_made, b * NB + n + AHEAD)
                    split_mm(C[:, 0, :], [
                        (arh[:, ft, :], arl[:, ft, :], xTh[:, ft, blk(n)], xTl[:, ft, blk(n)]) for ft in range(FT)]
                    ).then_inc(s1b_psum, 1)
                run_transpose(b, 0)
                spread_max(b, 0)
                pe.wait_ge(h_read, (b + 1) * MT + AHEAD)
                pe.wait_ge(h_ones, b + 1)
                gat(b, 0, True, False)
                with pe.Fori(1, NB - 1) as n:
                    gat(b, n, False, False)
                gat(b, NB - 1, False, True)


_INS = ["x", "adj", "L0_gnn_Wq", "L0_gnn_bq", "L0_gnn_Wk", "L0_gnn_bk", "L0_gnn_Wv", "L0_gnn_bv",
        "L0_gnn_Wo", "L0_gnn_bo", "L0_gnn_gamma", "L0_gnn_beta", "L1_gnn_W", "L1_gnn_a"]


def kernel(**inputs):
    import numpy as _np
    import concourse.bacc as _bacc
    from concourse import mybir as _mybir
    from concourse.bass_utils import run_bass_kernel_spmd as _run

    nc = _bacc.Bacc("TRN2", target_bir_lowering=False, num_devices=1)
    arrays, args = {}, []
    for name in _INS:
        a = _np.ascontiguousarray(inputs[name])
        arrays[f"in_{name}_dram"] = a
        args.append(nc.dram_tensor(f"in_{name}_dram", a.shape, _mybir.dt.from_np(a.dtype), kind="ExternalInput").ap())
    out = nc.dram_tensor("out_0_dram", inputs["x"].shape, _mybir.dt.float32, kind="ExternalOutput").ap()
    adj_resnorm_kernel(nc, *args, out)
    r = _run(nc, [arrays], core_ids=[0])
    return r.results[0]["out_0_dram"]
```

```python
from contextlib import ExitStack

import numpy as np
import concourse.bass as bass
from concourse import mybir

ALU = mybir.AluOpType
ACT = mybir.ActivationFunctionType
AX = mybir.AxisListType
F32 = mybir.dt.float32
F16 = mybir.dt.float16
BF16 = mybir.dt.bfloat16
I32 = mybir.dt.int32
RMAX = bass.bass_isa.ReduceOp.max

P = 128
WS = 64.0
EPS = 1e-5


def adj_resnorm_kernel(nc, x, adj, Wq, bq, Wk, bk, Wv, bv, Wo, bo, gamma, beta, W1, a1, out):
    B, N, F = x.shape
    H = 4
    DH = F // H
    FT = F // P
    MT = N // P
    BLK = 512
    NB = N // BLK
    NT = BLK // P
    CHUNK = 256
    KT = CHUNK // P
    CH = N // CHUNK
    STEPS = H * CH
    TB = NB * STEPS
    DV = DH + 1
    SC = float(np.sqrt(DH)) * WS * WS
    CLIP = 10.0 * SC
    GS = 2.0 ** -11
    SLOPE = 0.2
    SPLIT = [j for j in range(CH) if j % 2 == 0]
    NSPLIT = len(SPLIT)
    LIFT = 10.0 - 6.0 * float(np.log(2.0))
    assert N == MT * P and F == 256 and CLIP == 10.0 * 2 ** 15 and FT == 2

    with ExitStack() as ctx:
        def sb(name, shape, dt):
            return ctx.enter_context(nc.sbuf_tensor(name, shape, dt))

        def sem(name):
            return ctx.enter_context(nc.semaphore(name))

        limit = sb("limit", [P, MT, N], BF16)
        Q = sb("Q", [P, NB, H, BLK], F16)
        K1 = sb("K1", [P, H, N], F16)
        K2 = sb("K2", [P, H, N], F16)
        V = sb("V", [P, MT, H * DV], F32)
        probs = sb("probs", [P, 4, KT, BLK], F32)
        prest = sb("prest", [P, 2, KT, BLK], F16)
        xTh = sb("xTh", [P, FT, N], F16)
        xTl = sb("xTl", [P, FT, N], F16)
        xin = sb("xin", [P, NT, F], F32)
        xres = xin
        r1 = sb("r1", [P, NT, F], F32)
        x1t = sb("x1t", [P, NT, F], F32)
        ctxs = sb("ctxs", [P, NT, F], F32)
        cTh = sb("cTh", [P, FT, BLK], F16)
        cTl = sb("cTl", [P, FT, BLK], F16)
        osb = sb("osb", [P, 4, NT, DV], F32)
        rz = sb("rz", [P, 4, NT], F32)
        scaled = sb("scaled", [P, NT, DH], F32)
        WTh = sb("WTh", [P, 4, FT, F], F16)
        WTl = sb("WTl", [P, 4, FT, F], F16)
        W1h = sb("W1h", [P, FT, F + 2], F16)
        W1l = sb("W1l", [P, FT, F + 2], F16)
        arh = sb("arh", [P, FT, P], F16)
        arl = sb("arl", [P, FT, P], F16)
        rows = sb("rows", [P, 4, F], F32)
        bqk = sb("bqk", [P, 2, FT], F32)
        ident = sb("ident", [P, P], F32)
        identb = sb("identb", [P, P], BF16)
        ones = sb("ones", [P, P], F32)
        s12 = sb("s12", [P, MT, 2], F32)
        s2m = sb("s2m", [P, 2], F32)
        st = sb("st", [P, NT, 6], F32)
        mv = sb("mv", [P, NT, 2], F32)
        rs = sb("rs", [P, 2, NT], F32)
        mhalf = sb("mhalf", [P, NT], F32)
        lift = sb("lift", [P, 1], F32)
        msm = sb("msm", [P, 6, NT], F32)
        lrz = sb("lrz", [P, NT], F32)
        x1s = Q[:, :, :, :].rearrange("p a b c -> p (a b c)").bitcast(F32).rearrange(
            "p (b t f) -> p b t f", b=NB, t=NT)
        k1f = K1[:, :, :].rearrange("p a b -> p (a b)").bitcast(F32)
        k2f = K2[:, :, :].rearrange("p a b -> p (a b)").bitcast(F32)
        s1b = k1f[:, 0:N]
        mb = k1f[:, N:2 * N]
        run = k2f[:, 0:BLK]
        runs = [k2f[:, (2 + i) * BLK:(3 + i) * BLK] for i in range(2)]
        diag = k2f[:, BLK:2 * BLK].rearrange("p (t c) -> p t c", t=NT)
        pbf = probs[:, :, :, :].rearrange("p s i c -> p (s i c)").bitcast(BF16).rearrange(
            "p (s i c two) -> p s i c two", s=4, i=KT, two=2)[:, :, :, :, 1]
        Vp = V[:, :, :].rearrange("p m d -> p (m d)").bitcast(F16).rearrange(
            "p (m two h d) -> p m two h d", m=MT, two=2, h=H)
        vstage = r1
        adji = K1[:, :, :].rearrange("p a b -> p (a b)").bitcast(I32).rearrange("p (s n) -> p s n", s=2)
        adjb = K2[:, :, :].rearrange("p a b -> p (a b)").bitcast(BF16)[:, 0:2 * N].rearrange("p (s n) -> p s n", s=2)
        wst = Q[:, :, :, :].rearrange("p a b c -> p (a b c)").bitcast(F32)
        wnat = wst[:, 0:4 * FT * F].rearrange("p (w t f) -> p w t f", w=4, t=FT)
        w1f = wst[:, 2048:2048 + FT * (F + 2)].rearrange("p (t f) -> p t f", t=FT)
        abc = wst[:, 2600:2600 + 2 * F].rearrange("p (a f) -> p a f", a=2)
        wtmp = probs[:, 0, :, :].rearrange("p a c -> p (a c)").rearrange("p (a t f) -> p a t f", a=2, t=FT)

        S = ctx.enter_context(nc.psum_tensor("S", [P, 2, KT, BLK], F32))
        O = ctx.enter_context(nc.psum_tensor("O", [P, 2, BLK], F32))
        C = ctx.enter_context(nc.psum_tensor("C", [P, 2, BLK], F32))
        Sf = S[:, :, :, :].rearrange("p a b c -> p (a b) c")
        Sb = S[:, :, :, :].rearrange("p a b c -> p a (b c)").bitcast(BF16)
        Cn = C[:, :, :].rearrange("p a c -> p (a c)").rearrange("p (t f) -> p t f", t=NT)

        w_in, row_in, const_made = sem("w_in"), sem("row_in"), sem("const_made")
        wT_psum, wT_hi, wT_split = sem("wT_psum"), sem("wT_hi"), sem("wT_split")
        wa_made, w1_hi, w1_split, bias_made = sem("wa_made"), sem("w1_hi"), sem("w1_split"), sem("bias_made")
        adj_in = [sem("adj_in0"), sem("adj_in1")]
        adj_bf, adj_T, lim_act, lim_dve = sem("adj_bf"), sem("adj_T"), sem("lim_act"), sem("lim_dve")
        x_in, xT_psum, xT_hi, xT_split = sem("x_in"), sem("xT_psum"), sem("xT_hi"), sem("xT_split")
        q_psum, k_psum, v_psum = sem("q_psum"), sem("k_psum"), sem("v_psum")
        q_hi, k_hi, q_split, k_split = sem("q_hi"), sem("k_hi"), sem("q_split"), sem("k_split")
        k_swapped, v_made, v_ones = sem("k_swapped"), sem("v_made"), sem("v_ones")
        v_staged, v_value, v_split, rest_made = sem("v_staged"), sem("v_value"), sem("v_split"), sem("rest_made")
        scored, clipped, exped, pv_done = sem("scored"), sem("clipped"), sem("exped"), sem("pv_done")
        o_read, rz_made, mult_done, summed = sem("o_read"), sem("rz_made"), sem("mult_done"), sem("summed")
        cT_psum, cT_hi, cT_split = sem("cT_psum"), sem("cT_hi"), sem("cT_split")
        res_in, res_bo, res_made = sem("res_in"), sem("res_bo"), sem("res_made")
        mix_psum, mix_read = sem("mix_psum"), sem("mix_read")
        ln_stats = [sem(f"ln{i}_stats") for i in range(3)]
        ln_mean = [sem(f"ln{i}_mean") for i in range(3)]
        ln_eps = [sem(f"ln{i}_eps") for i in range(3)]
        ln_rstd = [sem(f"ln{i}_rstd") for i in range(3)]
        ln_done = [sem(f"ln{i}_done") for i in range(3)]
        y_mult, y_made = sem("y_mult"), sem("y_made")
        x1_saved, x1T_psum, x1T_hi, x1T_split = sem("x1_saved"), sem("x1T_psum"), sem("x1T_hi"), sem("x1T_split")
        h_psum, h_read, h_ones = sem("h_psum"), sem("h_read"), sem("h_ones")
        s1b_psum, s1b_made, s12_made = sem("s1b_psum"), sem("s1b_made"), sem("s12_made")
        s2m_part, s2m_made = sem("s2m_part"), sem("s2m_made")
        run_step, run_T, max_step = sem("run_step"), sem("run_T"), sem("max_step")
        lmax, diag_made = sem("lmax"), sem("diag_made")
        mb_psum, mb_made = sem("mb_psum"), sem("mb_made")
        g_summed, g_leaky, g_masked, g_shifted, g_exped = sem("g_summed"), sem("g_leaky"), sem("g_masked"), sem("g_shifted"), sem("g_exped")
        g_used, acc_done, lrz_made, acc_read = sem("g_used"), sem("acc_done"), sem("lrz_made"), sem("acc_read")
        stored = sem("stored")
        waits_over = sem("waits_over")

        AHEAD = 1
        from_ahead = (xT_psum, y_made, summed, cT_psum, x1T_psum, x1_saved, acc_done, stored, mix_psum, adj_T, run_T,
                      lim_act, lim_dve, s1b_made, q_split, k_split, v_made, x1T_split, h_read, mb_made, acc_read, v_split, pv_done, k_swapped)

        block = ctx.enter_context(nc.Block())
        MAXSTEPS = 6
        RUN_AT = [3, 3, 3, 3, 2, 2]

        def blk(n):
            return bass.ts(n, BLK)

        def n_whole(last_block):
            return [t for t in range(NT) if t // KT not in SPLIT]

        def apart(eng):
            eng.sem_inc(waits_over, 1)

        @block.sync
        def _(sp):
            for i, w in enumerate((Wq, Wk, Wv, Wo)):
                sp.dma_start(wnat[:, i, :, :], w.rearrange("(t p) f -> p t f", p=P)).then_inc(w_in, 16)
            sp.dma_start(w1f[:, :, 0:F], W1.rearrange("(t p) f -> p t f", p=P)).then_inc(w_in, 16)
            for i, r in enumerate((bv, bo, gamma, beta)):
                sp.dma_start(rows[:, i, :], r.rearrange("(a f) -> a f", a=1).to_broadcast([P, F])).then_inc(row_in, 16)
            for i in range(2):
                sp.dma_start(abc[:, i, :], a1[i * F:(i + 1) * F, :].rearrange("f a -> a f").to_broadcast([P, F])).then_inc(row_in, 16)
            for i, r in enumerate((bq, bk)):
                sp.dma_start(bqk[:, i, :], r.rearrange("(t p) -> p t", p=P), allow_slow_non_contiguous=True).then_inc(row_in, 16)
            adj_v = adj.rearrange("(t p) m -> t p m", p=P)
            for s in range(2):
                sp.dma_start(adji[:, s, :], adj_v[s]).then_inc(adj_in[s], 16)
            with sp.Fori(1, MT // 2) as i:
                for s in range(2):
                    sp.wait_ge(adj_bf, i * 2 + s - 1)
                    sp.dma_start(adji[:, s, :], adj_v[i * 2 + s]).then_inc(adj_in[s], 16)

            x_v = x.rearrange("b (k t p) f -> (b k) p t f", t=NT, p=P)
            out_v = out.rearrange("b (k t p) f -> (b k) p t f", t=NT, p=P)
            halves = (slice(0, 64), slice(64, 128))

            def load_x(b, n):
                sp.wait_ge(xT_psum, b * NB + n + AHEAD)
                sp.dma_start(xin[:, :, :], x_v[b * NB + n]).then_inc(x_in, 16)

            def swap_k(b, n):
                sp.wait_ge(k_split, b * NB + n + 1 + AHEAD)
                sp.wait_ge(k_swapped, (b * NB + n) * 32 + AHEAD)
                for i in range(2):
                    sp.dma_start(K2[halves[i], :, blk(n)], K1[halves[1 - i], :, blk(n)]).then_inc(k_swapped, 16)

            def batch(b, last):
                load_x(b, 1)
                with sp.Fori(0, NB - 2) as n:
                    load_x(b, n + 2)
                    swap_k(b, n)
                with sp.Fori(NB - 2, NB) as n:
                    swap_k(b, n)
                sp.wait_ge(xT_psum, (b + 1) * NB + AHEAD)
                apart(sp)
                with sp.Fori(0, NB) as n:
                    sp.wait_ge(y_made, b * NB + n + AHEAD)
                    sp.dma_start(xres[:, :, :], x_v[b * NB + n]).then_inc(res_in, 16)
                    sp.wait_ge(ln_done[1], b * NB + n + 1)
                    sp.dma_start(x1s[:, n, :, :], x1t[:, :, :]).then_inc(x1_saved, 16)
                if not last:
                    load_x(b + 1, 0)
                with sp.Fori(0, NB) as n:
                    sp.wait_ge(ln_done[2], b * NB + n + 1)
                    sp.dma_start(out_v[b * NB + n], x1t[:, :, :]).then_inc(stored, 16)

            load_x(0, 0)
            with sp.Fori(0, B - 1) as b:
                batch(b, False)
            batch(B - 1, True)
            sp.wait_ge(stored, B * NB * 16 + AHEAD)

        @block.gpsimd
        def _(pool):
            for s in from_ahead:
                pool.sem_inc(s, AHEAD)
            pool.memset(ident[:, :], 0.0).then_inc(const_made, 1)
            pool.memset(identb[:, :], 0.0).then_inc(const_made, 1)
            pool.memset(ones[:, :], 1.0).then_inc(const_made, 1)
            pool.memset(mhalf[:, :], -0.5).then_inc(const_made, 1)
            pool.memset(lift[:, :], LIFT).then_inc(const_made, 1)
            pool.wait_ge(const_made, 5)
            for m in (ident, identb):
                pool.affine_select(out=m[:, :], in_=m[:, :], compare_op=ALU.not_equal, fill=1.0,
                                   base=0, pattern=[[-1, P]], channel_multiplier=1).then_inc(const_made, 1)

            def rstd(kind, g):
                pool.wait_ge(ln_mean[kind], g + 1)
                apart(pool)
                pool.tensor_scalar(rs[:, 0, :], mv[:, :, 1], EPS, None, ALU.add).then_inc(ln_eps[kind], 1)
                pool.wait_ge(ln_eps[kind], g + 1)
                pool.tensor_tensor(rs[:, 1, :], rs[:, 0, :], mhalf[:, :], ALU.pow).then_inc(ln_rstd[kind], 1)

            def accumulate(b, n, s, head=False):
                t = b * TB + n * STEPS + s
                h, j, slot = s // CH, s % CH, s % 4
                dst = ctxs[:, :, h * DH:(h + 1) * DH]
                first = j == 0
                pool.wait_ge(summed, t + AHEAD)
                pool.wait_ge(rz_made, t + 1)
                if first and h == 0 and not head:
                    pool.wait_ge(cT_psum, (b * NB + n) * 2 - 1 + AHEAD)
                if first and h == 2:
                    pool.wait_ge(cT_psum, (b * NB + n) * 2 + AHEAD)
                o = pool.tensor_tensor(dst if first else scaled[:, :, :], osb[:, slot, :, 0:DH],
                                       rz[:, slot, :].unsqueeze(2).to_broadcast([P, NT, DH]), ALU.mult)
                if first:
                    o.then_inc(summed, 1)
                else:
                    o.then_inc(mult_done, 1)
                    pool.wait_ge(mult_done, (b * NB + n) * (STEPS - H) + s - h)
                    pool.tensor_tensor(dst, dst, scaled[:, :, :], ALU.add).then_inc(summed, 1)

            def bcast(i):
                return rows[:, i, :].unsqueeze(1).to_broadcast([P, NT, F])

            def residual_bo(g):
                pool.wait_ge(res_in, (g + 1) * 16)
                pool.wait_ge(x1T_psum, g + AHEAD)
                pool.wait_ge(x1_saved, g * 16 + AHEAD)
                pool.tensor_tensor(x1t[:, :, :], xres[:, :, :], bcast(1), ALU.add).then_inc(res_bo, 1)

            def residual_beta(g):
                pool.wait_ge(res_bo, g + 1)
                pool.tensor_tensor(xres[:, :, :], xres[:, :, :], bcast(3), ALU.add).then_inc(res_made, 1)

            def y_gamma(g):
                pool.wait_ge(ln_done[0], g + 1)
                pool.tensor_tensor(r1[:, :, :], r1[:, :, :], bcast(2), ALU.mult).then_inc(y_mult, 1)

            def y_residual(g):
                pool.wait_ge(y_mult, g + 1)
                pool.wait_ge(res_made, g + 1)
                pool.tensor_tensor(r1[:, :, :], r1[:, :, :], xres[:, :, :], ALU.add).then_inc(y_made, 1)

            pool_mix = {12: residual_bo, 15: residual_beta, 19: lambda g: rstd(0, g), 21: y_gamma, 23: y_residual,
                        27: lambda g: rstd(1, g)}

            def attend(b, n, first):
                for s in range(STEPS):
                    if s >= 3:
                        accumulate(b, n, s - 3, head=first)
                    elif not first:
                        accumulate(b, n - 1, STEPS + s - 3)
                    if not first and s in pool_mix:
                        pool_mix[s](b * NB + n - 1)

            def shift(b, n, j):
                k = b * NB * CH + n * CH + j
                pool.wait_ge(g_masked, k + 1)
                apart(pool)
                pool.tensor_tensor(probs[:, j % 4, :, :], probs[:, j % 4, :, :],
                                   mb[:, blk(n)].unsqueeze(1).to_broadcast([P, KT, BLK]),
                                   ALU.subtract).then_inc(g_shifted, 1)

            pool.wait_ge(row_in, 8 * 16)
            with pool.Fori(0, B) as b:
                pool.wait_ge(acc_done, b * NB * NT + AHEAD)
                vo = V[:, :, :].rearrange("p m (h d) -> p m h d", h=H)[:, :, :, DH]
                apart(pool)
                pool.memset(vo, 1.0).then_inc(v_ones, 1)
                pool.wait_ge(v_ones, b * 2 + 1)
                apart(pool)
                for j in SPLIT:
                    last = pool.memset(Vp[:, j * KT:(j + 1) * KT, 0, :, DH], 1.0)
                last.then_inc(v_ones, 1)

                def split_v(n, last_block):
                    g = b * NB + n
                    pool.wait_ge(v_made, g + 1 + AHEAD)
                    tiles = NT - len(n_whole(last_block))
                    src = vstage[:, 0:tiles, :].rearrange("p t (h d) -> p t h d", h=H)
                    apart(pool)
                    for t in range(tiles):
                        last = pool.tensor_copy(Vp[:, n * NT + t, 0, :, 0:DH], src[:, t, :, :])
                    last.then_inc(v_value, 1)
                    pool.wait_ge(v_value, g + 1)
                    apart(pool)
                    for t in range(tiles):
                        last = pool.tensor_tensor(Vp[:, n * NT + t, 1, :, 0:DH], src[:, t, :, :],
                                                  Vp[:, n * NT + t, 0, :, 0:DH], ALU.subtract)
                    last.then_inc(v_split, 1)
                with pool.Fori(0, NB - 1) as n:
                    split_v(n, False)
                split_v(NB - 1, True)
                pool.wait_ge(stored, b * NB * 16 + AHEAD)
                attend(b, 0, True)
                with pool.Fori(1, NB) as n:
                    attend(b, n, False)
                for s in range(3):
                    accumulate(b, NB - 1, STEPS + s - 3)
                for s in sorted(pool_mix):
                    pool_mix[s](b * NB + NB - 1)
                pool.wait_ge(pv_done, (b + 1) * TB + AHEAD)
                apart(pool)
                pool.memset(V[:, :, 0:1], 1.0).then_inc(h_ones, 1)
                pool.wait_ge(s2m_part, b + 1)
                apart(pool)
                pool.partition_all_reduce(s2m[:, 1:2], s2m[:, 0:1], P, RMAX).then_inc(s2m_made, 1)

                def gat(n, first):
                    pool.wait_ge(mb_made, b * NB + n + 1 + AHEAD)
                    for j in range(CH):
                        shift(b, n, j)
                        if j == 3 and not first:
                            rstd(2, b * NB + n - 1)
                gat(0, True)
                with pool.Fori(1, NB) as n:
                    gat(n, False)
                rstd(2, b * NB + NB - 1)

        @block.scalar
        def _(act):
            for i in range(4):
                act.wait_ge(wT_psum, i + 1)
                act.activation(WTh[:, i, :, :], Sf[:, i, :].rearrange("p (t f) -> p t f", t=FT), ACT.Copy, scale=WS).then_inc(wT_hi, 1)
            act.wait_ge(wa_made, 1)
            act.activation(W1h[:, :, :], w1f, ACT.Copy, scale=WS).then_inc(w1_hi, 1)
            act.activation(arh[:, :, :], w1f[:, :, F:F + 1].to_broadcast([P, FT, P]), ACT.Copy, scale=WS).then_inc(w1_hi, 1)
            with act.Fori(0, MT // 2) as i:
                act.wait_ge(adj_T, i * 2 + 1 + AHEAD)
                apart(act)
                act.activation(limit[:, :, bass.ds(i * (2 * P), P)], Sb[:, 0, :].rearrange("p (m c) -> p m c", m=MT),
                               ACT.Copy).then_inc(lim_act, 1)

            def split_hi(b, n):
                g = b * NB + n
                act.wait_ge(q_psum, g + 1)
                apart(act)
                for o in range(FT):
                    for r in range(2):
                        rr = slice(64 * r, 64 * r + 64)
                        last = act.activation(Q[rr, n, 2 * o + r, :], Sf[rr, o, :], ACT.Identity, bias=bqk[rr, 0, o:o + 1])
                last.then_inc(q_hi, 1)
                act.wait_ge(k_psum, g + 1)
                apart(act)
                for o in range(FT):
                    for r in range(2):
                        rr = slice(64 * r, 64 * r + 64)
                        last = act.activation(K1[rr, 2 * o + r, blk(n)], Sf[rr, 2 + o, :], ACT.Identity, bias=bqk[rr, 1, o:o + 1])
                last.then_inc(k_hi, 1)

            def xT_value(b, n):
                act.wait_ge(xT_psum, b * NB + n + 1 + AHEAD)
                apart(act)
                act.activation(xTh[:, :, blk(n)], C[:, :, :], ACT.Copy).then_inc(xT_hi, 1)

            def exps(b, n, s):
                t = b * TB + n * STEPS + s
                act.wait_ge(clipped, t + 1)
                act.activation(probs[:, s % 4, :, :], probs[:, s % 4, :, :], ACT.Exp,
                               scale=1.0 / SC, bias=lift[:, 0:1]).then_inc(exped, 1)

            def read_o(b, n, s, early=False):
                t = b * TB + n * STEPS + s
                act.wait_ge(pv_done, t + 1 + AHEAD)
                if not early:
                    act.wait_ge(summed, t - 3 + AHEAD)
                act.activation(osb[:, s % 4, :, :], O[:, s % 2, 0:NT * DV].rearrange("p (t d) -> p t d", t=NT), ACT.Copy).then_inc(o_read, 1)

            def mix_value(g, o):
                act.wait_ge(cT_psum, g * 2 + o + 1 + AHEAD)
                act.wait_ge(mix_psum, g + AHEAD)
                act.activation(cTh[:, o, :], C[:, o, :], ACT.Copy).then_inc(cT_hi, 1)

            def x1T_value(b, n):
                act.wait_ge(x1T_psum, b * NB + n + 1 + AHEAD)
                apart(act)
                act.activation(xTh[:, :, blk(n)], C[:, :, :], ACT.Copy).then_inc(x1T_hi, 1)

            def read_h(b, n):
                for i in range(NT):
                    act.wait_ge(h_psum, (b * NB + n) * NT + i + 1)
                    apart(act)
                    act.activation(V[:, n * NT + i, 1:F + 3], Sf[:, i, 0:F + 2], ACT.Copy, scale=1.0 / WS).then_inc(h_read, 1)
                act.wait_ge(s1b_psum, b * NB + n + 1)
                apart(act)
                act.activation(s1b[:, blk(n)], C[:, 0, :], ACT.Copy, scale=GS / WS).then_inc(s1b_made, 1)

            def attend(b, n, first):
                for s in range(STEPS):
                    exps(b, n, s)
                    if s >= 2:
                        read_o(b, n, s - 2, early=first and s < 6)
                    elif not first:
                        read_o(b, n - 1, STEPS + s - 2)
                    if s in (3, 8) and not first:
                        mix_value(b * NB + n - 1, s // 8)
                    if s == 30 and not first:
                        x1T_value(b, n - 1)

            def pair_sum(b, n, j, early):
                if not early:
                    if j < 3:
                        act.wait_ge(g_used, (b * NB + n - 1) * (CH - 1) + j + 5)
                    elif j == 3:
                        act.wait_ge(acc_done, (b * NB + n) * NT + AHEAD)
                    else:
                        act.wait_ge(g_used, (b * NB + n) * (CH - 1) + j - 3)
                elif j > 3:
                    act.wait_ge(g_used, (b * NB + n) * (CH - 1) + j - 3)
                apart(act)
                for i in range(KT):
                    m = j * KT + i
                    last = act.activation(probs[:, j % 4, i, :], s1b[:, blk(n)], ACT.Identity, bias=s12[:, m, 1:2])
                last.then_inc(g_summed, 1)

            def read_mb(b, n):
                act.wait_ge(mb_psum, b * NB + n + 1)
                apart(act)
                act.activation(mb[:, blk(n)], O[:, 1, :], ACT.Copy).then_inc(mb_made, 1)

            def gat(b, n, first, last):
                for j in range(CH):
                    if j + 2 < CH:
                        pair_sum(b, n, j + 2, first)
                    elif not last:
                        pair_sum(b, n + 1, j + 2 - CH, False)
                    if j == CH - 1 and not last:
                        read_mb(b, n + 1)
                    k = (b * NB + n) * CH + j
                    act.wait_ge(g_shifted, k + 1)
                    act.activation(probs[:, j % 4, :, :], probs[:, j % 4, :, :], ACT.Exp, scale=1.0 / GS).then_inc(g_exped, 1)

            act.wait_ge(bias_made, 1)
            act.wait_ge(const_made, 7)
            with act.Fori(0, B) as b:
                xT_value(b, 0)
                with act.Fori(0, NB - 1) as n:
                    xT_value(b, n + 1)
                    split_hi(b, n)
                split_hi(b, NB - 1)
                attend(b, 0, True)
                with act.Fori(1, NB) as n:
                    attend(b, n, False)
                for s in range(2):
                    read_o(b, NB - 1, STEPS + s - 2)
                for o in range(FT):
                    mix_value(b * NB + NB - 1, o)
                with act.Fori(0, NB - 1) as n:
                    read_h(b, n)
                x1T_value(b, NB - 1)
                read_h(b, NB - 1)
                act.wait_ge(s1b_made, (b + 1) * NB + AHEAD)
                act.wait_ge(s12_made, b * 2 + 2)
                for j in range(2):
                    pair_sum(b, 0, j, True)
                read_mb(b, 0)
                gat(b, 0, True, False)
                with act.Fori(1, NB - 1) as n:
                    gat(b, n, False, False)
                gat(b, NB - 1, False, True)

        @block.vector
        def _(dve):
            for i in range(4):
                dve.wait_ge(wT_hi, i + 1)
                dve.scalar_tensor_tensor(WTl[:, i, :, :], Sf[:, i, :].rearrange("p (t f) -> p t f", t=FT), WS, WTh[:, i, :, :],
                                         ALU.mult, ALU.subtract).then_inc(wT_split, 1)
            dve.wait_ge(w_in, 5 * 16)
            dve.wait_ge(row_in, 8 * 16)
            for t in range(FT):
                for i in range(2):
                    last = dve.tensor_tensor(wtmp[:, i, t, :], w1f[:, t, 0:F], abc[:, i, :], ALU.mult)
            last.then_inc(run_step, 1)
            dve.wait_ge(run_step, 1)
            for i in range(2):
                last = dve.tensor_reduce(w1f[:, :, F + i], wtmp[:, i, :, :], AX.X, ALU.add)
            last.then_inc(wa_made, 1)
            dve.tensor_scalar(bqk[:, :, :], bqk[:, :, :], WS, None, ALU.mult).then_inc(bias_made, 1)
            dve.wait_ge(w1_hi, 2)
            dve.scalar_tensor_tensor(W1l[:, :, :], w1f, WS, W1h[:, :, :], ALU.mult, ALU.subtract).then_inc(w1_split, 1)
            dve.scalar_tensor_tensor(arl[:, :, :], w1f[:, :, F:F + 1].to_broadcast([P, FT, P]), WS, arh[:, :, :],
                                     ALU.mult, ALU.subtract).then_inc(w1_split, 1)

            def to_limit(i, s):
                dve.wait_ge(adj_in[s], i * 16 + 16)
                dve.wait_ge(adj_T, i * 2 + AHEAD)
                dve.tensor_scalar(adjb[:, s, :], adji[:, s, :], 2 * CLIP, -CLIP, ALU.mult, ALU.add).then_inc(adj_bf, 1)

            with dve.Fori(0, MT // 2) as i:
                to_limit(i, 0)
                to_limit(i, 1)
                dve.wait_ge(adj_T, i * 2 + 2 + AHEAD)
                dve.tensor_copy(limit[:, :, bass.ds(i * (2 * P) + P, P)], Sb[:, 1, :].rearrange("p (m c) -> p m c", m=MT)).then_inc(lim_dve, 1)

            def xT_rest(b, n):
                dve.wait_ge(xT_hi, b * NB + n + 1)
                dve.tensor_tensor(xTl[:, :, blk(n)], C[:, :, :], xTh[:, :, blk(n)], ALU.subtract).then_inc(xT_split, 1)

            def split_rest(b, n, last_block=False):
                g = b * NB + n
                for w, ready, done in ((0, q_hi, q_split), (1, k_hi, k_split)):
                    dve.wait_ge(ready, g + 1)
                    for o in range(FT):
                        for r in range(2):
                            rr = slice(64 * r, 64 * r + 64)
                            ll = slice(64 - 64 * r, 128 - 64 * r)
                            val = (lambda s: Q[s, n, 2 * o + r, :] if w == 0 else K1[s, 2 * o + r, blk(n)])
                            last = dve.scalar_tensor_tensor(val(ll), Sf[rr, 2 * w + o, :], bqk[rr, w, o:o + 1], val(rr),
                                                            ALU.add, ALU.subtract)
                    last.then_inc(done, 1)
                dve.wait_ge(v_psum, g + 1)
                dve.wait_ge(v_split, g + AHEAD)
                apart(dve)
                whole = n_whole(last_block)
                for t in range(NT):
                    dst = (V[:, n * NT + t, :].rearrange("p (h d) -> p h d", h=H)[:, :, 0:DH] if t in whole else
                           vstage[:, t, :].rearrange("p (h d) -> p h d", h=H))
                    last = dve.scalar_tensor_tensor(
                        dst, O[:, t // 2, (t % 2) * F:(t % 2 + 1) * F].rearrange("p (h d) -> p h d", h=H), 1.0 / WS,
                        rows[:, 0, :].rearrange("p (h d) -> p h d", h=H), ALU.mult, ALU.add)
                last.then_inc(v_made, 1)

            def clip(b, n, s):
                t = b * TB + n * STEPS + s
                j = s % CH
                dve.wait_ge(scored, t + 1)
                dve.scalar_tensor_tensor(probs[:, s % 4, :, :], S[:, s % 2, :, :], -CLIP,
                                         limit[:, j * KT:(j + 1) * KT, blk(n)], ALU.max, ALU.min).then_inc(clipped, 1)

            def rest(b, n, s):
                t = b * TB + n * STEPS + s
                h, j = s // CH, s % CH
                if j in SPLIT:
                    dve.wait_ge(exped, t + 1)
                    dve.wait_ge(pv_done, t - 1 + AHEAD)
                    dve.tensor_tensor(prest[:, s % 2, :, :], probs[:, s % 4, :, :], pbf[:, s % 4, :, :],
                                      ALU.subtract).then_inc(rest_made, 1)

            def recip(b, n, s):
                t = b * TB + n * STEPS + s
                dve.wait_ge(o_read, t + 1)
                dve.reciprocal(rz[:, s % 4, :], osb[:, s % 4, :, DH]).then_inc(rz_made, 1)

            def stats(kind, g):
                for t in range(NT):
                    last = dve.bn_stats(st[:, t, :], r1[:, t, :])
                last.then_inc(ln_stats[kind], 1)

            def mean(kind, g):
                dve.wait_ge(ln_stats[kind], g + 1)
                apart(dve)
                for t in range(NT):
                    last = dve.bn_aggr(mv[:, t, :], st[:, t, :])
                last.then_inc(ln_mean[kind], 1)

            def normalise(kind, g, dst):
                dve.wait_ge(ln_rstd[kind], g + 1)
                for t in range(NT):
                    last = dve.tensor_scalar(dst[:, t, :], r1[:, t, :], mv[:, t, 0:1], rs[:, 1, t:t + 1], ALU.subtract, ALU.mult)
                last.then_inc(ln_done[kind], 1)

            def mix_rest(g, o):
                dve.wait_ge(cT_hi, g * 2 + o + 1)
                dve.tensor_tensor(cTl[:, o, :], C[:, o, :], cTh[:, o, :], ALU.subtract).then_inc(cT_split, 1)

            def mix_add(g):
                dve.wait_ge(mix_psum, g + 1 + AHEAD)
                dve.wait_ge(res_bo, g + 1)
                dve.scalar_tensor_tensor(r1[:, :, :], Cn, 1.0 / WS, x1t[:, :, :], ALU.mult, ALU.add).then_inc(mix_read, 1)

            def mix_stats1(g):
                dve.wait_ge(mix_read, g + 1)
                stats(0, g)

            def mix_stats2(g):
                dve.wait_ge(y_made, g + 1 + AHEAD)
                stats(1, g)

            dve_mix = {4: lambda g: mix_rest(g, 0), 10: lambda g: mix_rest(g, 1), 14: mix_add, 16: mix_stats1,
                       18: lambda g: mean(0, g), 20: lambda g: normalise(0, g, r1), 24: mix_stats2,
                       26: lambda g: mean(1, g), 28: lambda g: normalise(1, g, x1t)}

            def x1T_rest(b, n):
                dve.wait_ge(x1T_hi, b * NB + n + 1)
                dve.tensor_tensor(xTl[:, :, blk(n)], C[:, :, :], xTh[:, :, blk(n)], ALU.subtract).then_inc(x1T_split, 1)

            def attend(b, n, first):
                for s in range(STEPS):
                    clip(b, n, s)
                    if s >= 1:
                        rest(b, n, s - 1)
                    elif not first:
                        rest(b, n - 1, STEPS - 1)
                    if s >= 3:
                        recip(b, n, s - 3)
                    elif not first:
                        recip(b, n - 1, STEPS + s - 3)
                    if not first and s in dve_mix:
                        dve_mix[s](b * NB + n - 1)
                    if not first and s == STEPS - 1:
                        x1T_rest(b, n - 1)

            def run_max(b, n, m):
                before = (b * NB + n) * (MT + 1) + 1
                r = runs[m % 2]
                if m < 2:
                    dve.wait_ge(run_T, b * NB + n + AHEAD)
                    dve.wait_ge(run_step, before)
                    dve.tensor_scalar(r, limit[:, m, blk(n)], s12[:, m, 1:2], None, ALU.min).then_inc(run_step, 1)
                else:
                    dve.wait_ge(run_step, before + m - 1)
                    dve.scalar_tensor_tensor(r, limit[:, m, blk(n)], s12[:, m, 1:2], r, ALU.min, ALU.max).then_inc(run_step, 1)
                if m == MT - 1:
                    dve.wait_ge(run_step, before + MT)
                    dve.tensor_tensor(run, runs[0], runs[1], ALU.max).then_inc(run_step, 1)

            def node_scores(b, m0, m1):
                dve.wait_ge(h_read, b * MT + m1 + AHEAD)
                dve.tensor_scalar(s12[:, m0:m1, :], V[:, m0:m1, F + 1:F + 3], GS, None, ALU.mult).then_inc(s12_made, 1)
                dve.wait_ge(s12_made, b * 2 + (2 if m1 == MT else 1))

            def row_max(b, n):
                g = b * NB + n
                G, some, cand, sel, lk, M = (msm[:, i, :] for i in range(6))
                steps = [0]

                def link(o):
                    steps[0] += 1
                    o.then_inc(max_step, 1)
                    dve.wait_ge(max_step, g * MAXSTEPS + steps[0])

                dve.wait_ge(run_T, g + 1 + AHEAD)
                link(dve.tensor_reduce(G, O[:, 0, :].rearrange("p (t c) -> p t c", t=NT), AX.X, ALU.max))
                link(dve.tensor_scalar(some, G, -CLIP, None, ALU.is_gt))
                link(dve.scalar_tensor_tensor(cand, some, -2.0 ** 60, s2m[:, 1:2].to_broadcast([P, NT]), ALU.mult, ALU.add))
                link(dve.tensor_tensor(sel, G, cand, ALU.max))
                link(dve.tensor_tensor(lk, s12[:, bass.ts(n, NT), 0], sel, ALU.add))
                dve.tensor_scalar(some, some, CLIP, -CLIP, ALU.mult, ALU.add)
                link(dve.scalar_tensor_tensor(M, lk, SLOPE, lk, ALU.mult, ALU.max))
                dve.tensor_tensor(M, M, some, ALU.add).then_inc(lmax, 1)
                dve.wait_ge(lmax, g + 1)
                dve.tensor_tensor(diag, ident[:, :].unsqueeze(1).to_broadcast([P, NT, P]),
                                  M.unsqueeze(2).to_broadcast([P, NT, P]), ALU.mult).then_inc(diag_made, 1)

            def finish(b, n):
                g = b * NB + n
                for t in range(NT):
                    dve.wait_ge(acc_done, g * NT + t + 1 + AHEAD)
                    dve.reciprocal(lrz[:, t:t + 1], Sf[:, t, 0:1]).then_inc(lrz_made, 1)
                    dve.wait_ge(lrz_made, g * NT + t + 1)
                    dve.scalar_tensor_tensor(r1[:, t, :], Sf[:, t, 1:F + 1], lrz[:, t:t + 1], x1s[:, n, t, :],
                                             ALU.mult, ALU.add).then_inc(acc_read, 1)

            def finish_stats(g):
                dve.wait_ge(acc_read, (g + 1) * NT + AHEAD)
                stats(2, g)

            def finish_norm(g):
                dve.wait_ge(stored, g * 16 + AHEAD)
                normalise(2, g, x1t)

            def gat(b, n, first, last):
                m = 0
                for j in range(CH):
                    k = (b * NB + n) * CH + j
                    w = probs[:, j % 4, :, :]
                    dve.wait_ge(g_summed, k + 1)
                    dve.scalar_tensor_tensor(w, w, SLOPE, w, ALU.mult, ALU.max).then_inc(g_leaky, 1)
                    dve.wait_ge(g_leaky, k + 1)
                    dve.scalar_tensor_tensor(w, limit[:, j * KT:(j + 1) * KT, blk(n)], 0.0,
                                             w, ALU.min, ALU.add).then_inc(g_masked, 1)
                    if not first:
                        if j == 1:
                            finish(b, n - 1)
                        if j == 2:
                            finish_stats(b * NB + n - 1)
                        if j == 3:
                            mean(2, b * NB + n - 1)
                        if j == 5:
                            finish_norm(b * NB + n - 1)
                    if not last:
                        if j < len(RUN_AT):
                            for _ in range(RUN_AT[j]):
                                run_max(b, n + 1, m)
                                m += 1
                        if j == 6:
                            row_max(b, n + 1)

            with dve.Fori(0, B) as b:
                xT_rest(b, 0)
                with dve.Fori(0, NB - 1) as n:
                    xT_rest(b, n + 1)
                    split_rest(b, n)
                split_rest(b, NB - 1, True)
                attend(b, 0, True)
                with dve.Fori(1, NB) as n:
                    attend(b, n, False)
                rest(b, NB - 1, STEPS - 1)
                for s in range(3):
                    recip(b, NB - 1, STEPS + s - 3)
                last_g = b * NB + NB - 1
                early = (NB - 1) * NT
                for s in sorted(dve_mix):
                    dve_mix[s](last_g)
                    if s == 18:
                        node_scores(b, 0, early)
                        for m in range(early // 2):
                            run_max(b, 0, m)
                    if s == 20:
                        for m in range(early // 2, early):
                            run_max(b, 0, m)
                x1T_rest(b, NB - 1)
                node_scores(b, early, MT)
                dve.tensor_reduce(s2m[:, 0:1], s12[:, :, 1], AX.X, ALU.max).then_inc(s2m_part, 1)
                for m in range(early, MT):
                    run_max(b, 0, m)
                dve.wait_ge(x1_saved, (b + 1) * NB * 16 + AHEAD)
                dve.wait_ge(s2m_made, b + 1)
                row_max(b, 0)
                gat(b, 0, True, False)
                with dve.Fori(1, NB - 1) as n:
                    gat(b, n, False, False)
                gat(b, NB - 1, False, True)
                finish(b, NB - 1)
                finish_stats(b * NB + NB - 1)
                mean(2, b * NB + NB - 1)
                finish_norm(b * NB + NB - 1)

        @block.tensor
        def _(pe):
            pe.wait_ge(const_made, 7)
            pe.wait_ge(w_in, 5 * 16)
            for i in range(4):
                for ft in range(FT):
                    for ot in range(FT):
                        last = pe.transpose(Sf[:, i, ft * F + ot * P:ft * F + (ot + 1) * P], wnat[:, i, ot, ft * P:(ft + 1) * P], ident[:, :])
                last.then_inc(wT_psum, 1)
            pe.wait_ge(wT_split, 4)
            with pe.Fori(0, MT // 2) as i:
                for s, lim in ((0, lim_act), (1, lim_dve)):
                    pe.wait_ge(adj_bf, i * 2 + s + 1)
                    pe.wait_ge(lim, i + AHEAD)
                    for m in range(MT):
                        last = pe.transpose(Sb[:, s, m * P:(m + 1) * P], adjb[:, s, m * P:(m + 1) * P], identb[:, :])
                    last.then_inc(adj_T, 1)

            def split_mm(dst, pairs):
                ops = [(lh, rh) for (lh, ll, rh, rl) in pairs] + [(lh, rl) for (lh, ll, rh, rl) in pairs] + \
                      [(ll, rh) for (lh, ll, rh, rl) in pairs]
                for i, (w, m) in enumerate(ops):
                    last = pe.matmul(dst, lhsT=w, rhs=m, start=i == 0, stop=i == len(ops) - 1)
                return last

            def xT(b, n, head):
                g = b * NB + n
                pe.wait_ge(x_in, g * 16 + 16)
                if head:
                    pe.wait_ge(s1b_made, b * NB + AHEAD)
                else:
                    pe.wait_ge(xT_split, g)
                for ft in range(FT):
                    for t in range(NT):
                        last = pe.transpose(C[:, ft, t * P:(t + 1) * P], xin[:, t, ft * P:(ft + 1) * P], ident[:, :])
                last.then_inc(xT_psum, 1)

            def qkv(b, n, head):
                g = b * NB + n
                pe.wait_ge(xT_split, g + 1)
                for w, psum, free in ((0, q_psum, q_split), (1, k_psum, k_split)):
                    pe.wait_ge(free, g + AHEAD)
                    for o in range(FT):
                        last = split_mm(Sf[:, 2 * w + o, :], [
                            (WTh[:, w, ft, o * P:(o + 1) * P], WTl[:, w, ft, o * P:(o + 1) * P],
                             xTh[:, ft, blk(n)], xTl[:, ft, blk(n)]) for ft in range(FT)])
                    last.then_inc(psum, 1)
                pe.wait_ge(v_made, g + AHEAD)
                for t in range(NT):
                    cols = bass.ds(n * BLK + t * P, P)
                    last = split_mm(O[:, t // 2, (t % 2) * F:(t % 2 + 1) * F], [
                        (xTh[:, ft, cols], xTl[:, ft, cols], WTh[:, 2, ft, :], WTl[:, 2, ft, :]) for ft in range(FT)])
                last.then_inc(v_psum, 1)

            def score(b, n, s, head=False):
                t = b * TB + n * STEPS + s
                h, j = s // CH, s % CH
                if isinstance(n, int) and h == 0 and j * KT % NT == 0:
                    pe.wait_ge(k_swapped, (b * NB + j * KT // NT + 1) * 32 + AHEAD)
                if not head:
                    pe.wait_ge(clipped, t - 1)
                for i in range(KT):
                    m = j * KT + i
                    for r, K in enumerate((K1, K2)):
                        last = pe.matmul(S[:, s % 2, i, :], lhsT=K[:, h, m * P:(m + 1) * P], rhs=Q[:, n, h, :],
                                         start=r == 0, stop=r == 1)
                last.then_inc(scored, 1)

            def pv(b, n, s, head=False):
                t = b * TB + n * STEPS + s
                h, j = s // CH, s % CH
                if isinstance(n, int) and h == 0 and j * KT % NT == 0:
                    pe.wait_ge(v_split, b * NB + j * KT // NT + 1 + AHEAD)
                if j in SPLIT:
                    pe.wait_ge(rest_made, ((b * NB + n) * H + h) * NSPLIT + SPLIT.index(j) + 1)
                else:
                    pe.wait_ge(exped, t + 1)
                if not head:
                    pe.wait_ge(o_read, t - 1)
                for q in range(NT):
                    cols = slice(q * P, (q + 1) * P)
                    for i in range(KT):
                        m = j * KT + i
                        o = O[:, s % 2, q * DV:(q + 1) * DV]
                        if j in SPLIT:
                            for r, w in enumerate((pbf[:, s % 4, i, cols], prest[:, s % 2, i, cols])):
                                pe.matmul(o, lhsT=w, rhs=Vp[:, m, 0, h, :], start=i == 0 and r == 0, stop=False)
                                last = pe.matmul(o[:, 0:DH], lhsT=w, rhs=Vp[:, m, 1, h, 0:DH], start=False,
                                                 stop=i == KT - 1 and r == 1)
                        else:
                            last = pe.matmul(o, lhsT=probs[:, s % 4, i, cols], rhs=V[:, m, h * DV:(h + 1) * DV],
                                             start=i == 0, stop=i == KT - 1)
                last.then_inc(pv_done, 1)

            def mix_T(b, n, o):
                g = b * NB + n
                pe.wait_ge(summed, b * TB + n * STEPS + (o + 1) * STEPS // 2 + AHEAD)
                if o == 0:
                    pe.wait_ge(x1T_split, g + AHEAD)
                for t in range(NT):
                    last = pe.transpose(C[:, o, t * P:(t + 1) * P], ctxs[:, t, o * P:(o + 1) * P], ident[:, :])
                last.then_inc(cT_psum, 1)

            def mix_project(b, n):
                g = b * NB + n
                pe.wait_ge(cT_split, g * 2 + 2)
                for t in range(NT):
                    last = split_mm(Cn[:, t, :], [
                        (cTh[:, o, t * P:(t + 1) * P], cTl[:, o, t * P:(t + 1) * P], WTh[:, 3, o, :], WTl[:, 3, o, :])
                        for o in range(FT)])
                last.then_inc(mix_psum, 1)

            def x1T(b, n):
                pe.wait_ge(ln_done[1], b * NB + n + 1)
                if isinstance(n, int):
                    pe.wait_ge(s1b_made, b * NB + n + AHEAD)
                for ft in range(FT):
                    for t in range(NT):
                        last = pe.transpose(C[:, ft, t * P:(t + 1) * P], x1t[:, t, ft * P:(ft + 1) * P], ident[:, :])
                last.then_inc(x1T_psum, 1)

            pe_mix = {2: lambda b, n: mix_T(b, n, 0), 7: lambda b, n: mix_T(b, n, 1), 11: mix_project, 29: x1T}

            def attend(b, n, first):
                for s in range(STEPS):
                    score(b, n, s, head=first and s < 2)
                    if s >= 2:
                        pv(b, n, s - 2, head=first and s < 4)
                    elif not first:
                        pv(b, n - 1, STEPS + s - 2)
                    if not first and s in pe_mix:
                        pe_mix[s](b, n - 1)

            def gat_sum(b, n, j, head):
                k = (b * NB + n) * CH + j
                pe.wait_ge(g_exped, k + 1)
                for q in range(NT):
                    if j == 0 and not head:
                        pe.wait_ge(acc_read, (b * NB + n - 1) * NT + q + 1 + AHEAD)
                    for i in range(KT):
                        last = pe.matmul(Sf[:, q, 0:F + 1], lhsT=probs[:, j % 4, i, q * P:(q + 1) * P],
                                         rhs=V[:, j * KT + i, 0:F + 1], start=j == 0 and i == 0,
                                         stop=j == CH - 1 and i == KT - 1)
                    if j == CH - 1:
                        last.then_inc(acc_done, 1)
                if j < CH - 1:
                    last.then_inc(g_used, 1)

            def run_transpose(b, n):
                pe.wait_ge(run_step, (b * NB + n + 1) * (MT + 1) + 1)
                for t in range(NT):
                    last = pe.transpose(O[:, 0, t * P:(t + 1) * P], run[:, t * P:(t + 1) * P], ident[:, :])
                last.then_inc(run_T, 1)

            def spread_max(b, n):
                pe.wait_ge(diag_made, b * NB + n + 1)
                pe.wait_ge(mb_made, b * NB + n + AHEAD)
                pe.matmul(O[:, 1, :], lhsT=ones[:, :], rhs=k2f[:, BLK:2 * BLK], start=True, stop=True).then_inc(mb_psum, 1)

            def gat(b, n, first, last):
                for j in range(CH):
                    if not last and j == 6:
                        run_transpose(b, n + 1)
                    if not last and j == 7:
                        spread_max(b, n + 1)
                    gat_sum(b, n, j, first)

            def gat_h(b, n):
                pe.wait_ge(x1T_split, b * NB + n + 1 + AHEAD)
                for t in range(NT):
                    pe.wait_ge(h_read, (b * NB + n) * NT + AHEAD)
                    cols = bass.ds(n * BLK + t * P, P)
                    split_mm(Sf[:, t, 0:F + 2], [
                        (xTh[:, ft, cols], xTl[:, ft, cols], W1h[:, ft, :], W1l[:, ft, :]) for ft in range(FT)]
                    ).then_inc(h_psum, 1)
                pe.wait_ge(s1b_made, b * NB + n + AHEAD)
                pe.wait_ge(mix_read, (b + 1) * NB)
                split_mm(C[:, 0, :], [
                    (arh[:, ft, :], arl[:, ft, :], xTh[:, ft, blk(n)], xTl[:, ft, blk(n)]) for ft in range(FT)]
                ).then_inc(s1b_psum, 1)

            pe.wait_ge(w1_split, 2)
            with pe.Fori(0, B) as b:
                pe.wait_ge(acc_read, b * MT + AHEAD)
                xT(b, 0, True)
                with pe.Fori(0, NB - 1) as n:
                    xT(b, n + 1, False)
                    qkv(b, n, False)
                qkv(b, NB - 1, False)
                pe.wait_ge(q_split, (b + 1) * NB + AHEAD)
                pe.wait_ge(v_made, (b + 1) * NB + AHEAD)
                pe.wait_ge(v_ones, (b + 1) * 2)
                pe.wait_ge(lim_act, MT // 2 + AHEAD)
                pe.wait_ge(lim_dve, MT // 2 + AHEAD)
                attend(b, 0, True)
                with pe.Fori(1, NB) as n:
                    attend(b, n, False)
                for s in range(2):
                    pv(b, NB - 1, STEPS + s - 2)
                for s in (2, 7, 11):
                    pe_mix[s](b, NB - 1)
                with pe.Fori(0, NB - 1) as n:
                    gat_h(b, n)
                x1T(b, NB - 1)
                gat_h(b, NB - 1)
                run_transpose(b, 0)
                spread_max(b, 0)
                pe.wait_ge(h_read, (b + 1) * MT + AHEAD)
                pe.wait_ge(h_ones, b + 1)
                gat(b, 0, True, False)
                with pe.Fori(1, NB - 1) as n:
                    gat(b, n, False, False)
                gat(b, NB - 1, False, True)


_INS = ["x", "adj", "L0_gnn_Wq", "L0_gnn_bq", "L0_gnn_Wk", "L0_gnn_bk", "L0_gnn_Wv", "L0_gnn_bv",
        "L0_gnn_Wo", "L0_gnn_bo", "L0_gnn_gamma", "L0_gnn_beta", "L1_gnn_W", "L1_gnn_a"]


def kernel(**inputs):
    import numpy as _np
    import concourse.bacc as _bacc
    from concourse import mybir as _mybir
    from concourse.bass_utils import run_bass_kernel_spmd as _run

    nc = _bacc.Bacc("TRN2", target_bir_lowering=False, num_devices=1)
    arrays, args = {}, []
    for name in _INS:
        a = _np.ascontiguousarray(inputs[name])
        arrays[f"in_{name}_dram"] = a
        args.append(nc.dram_tensor(f"in_{name}_dram", a.shape, _mybir.dt.from_np(a.dtype), kind="ExternalInput").ap())
    out = nc.dram_tensor("out_0_dram", inputs["x"].shape, _mybir.dt.float32, kind="ExternalOutput").ap()
    adj_resnorm_kernel(nc, *args, out)
    r = _run(nc, [arrays], core_ids=[0])
    return r.results[0]["out_0_dram"]
```

```python
from contextlib import ExitStack

import numpy as np
import concourse.bass as bass
from concourse import mybir

ALU = mybir.AluOpType
ACT = mybir.ActivationFunctionType
AX = mybir.AxisListType
F32 = mybir.dt.float32
F16 = mybir.dt.float16
BF16 = mybir.dt.bfloat16
I32 = mybir.dt.int32
RMAX = bass.bass_isa.ReduceOp.max

P = 128
WS = 64.0
EPS = 1e-5


def adj_resnorm_kernel(nc, x, adj, Wq, bq, Wk, bk, Wv, bv, Wo, bo, gamma, beta, W1, a1, out):
    B, N, F = x.shape
    H = 4
    DH = F // H
    FT = F // P
    MT = N // P
    BLK = 512
    NB = N // BLK
    NT = BLK // P
    CHUNK = 256
    KT = CHUNK // P
    CH = N // CHUNK
    STEPS = H * CH
    TB = NB * STEPS
    DV = DH + 1
    SC = float(np.sqrt(DH)) * WS * WS
    CLIP = 10.0 * SC
    GS = 2.0 ** -11
    SLOPE = 0.2
    SPLIT = [j for j in range(CH) if j % 2 == 0 or j == CH - 1]
    POOL_REST = CH - 1
    DVE_REST = [j for j in SPLIT if j != POOL_REST]
    NREST = len(DVE_REST)
    LAG = 3
    LIFT = 10.0 - 6.0 * float(np.log(2.0))
    assert N == MT * P and F == 256 and CLIP == 10.0 * 2 ** 15 and FT == 2

    with ExitStack() as ctx:
        def sb(name, shape, dt):
            return ctx.enter_context(nc.sbuf_tensor(name, shape, dt))

        def sem(name):
            return ctx.enter_context(nc.semaphore(name))

        limit = sb("limit", [P, MT, N], BF16)
        Q = sb("Q", [P, NB, H, BLK], F16)
        K1 = sb("K1", [P, H, N], F16)
        K2 = sb("K2", [P, H, N], F16)
        V = sb("V", [P, MT, H * DV], F32)
        probs = sb("probs", [P, 4, KT, BLK], F32)
        prest = sb("prest", [P, 3, KT, BLK], F16)
        xTh = sb("xTh", [P, FT, N], F16)
        xTl = sb("xTl", [P, FT, N], F16)
        xin = sb("xin", [P, NT, F], F32)
        xres = xin
        r1 = sb("r1", [P, NT, F], F32)
        x1t = sb("x1t", [P, NT, F], F32)
        ctxs = sb("ctxs", [P, NT, F], F32)
        cTh = sb("cTh", [P, FT, BLK], F16)
        cTl = sb("cTl", [P, FT, BLK], F16)
        osb = sb("osb", [P, 4, NT, DV], F32)
        rz = sb("rz", [P, 4, NT], F32)
        scaled = sb("scaled", [P, NT, DH], F32)
        WTh = sb("WTh", [P, 4, FT, F], F16)
        WTl = sb("WTl", [P, 4, FT, F], F16)
        W1h = sb("W1h", [P, FT, F + 2], F16)
        W1l = sb("W1l", [P, FT, F + 2], F16)
        arh = sb("arh", [P, FT, P], F16)
        arl = sb("arl", [P, FT, P], F16)
        rows = sb("rows", [P, 4, F], F32)
        bqk = sb("bqk", [P, 2, FT], F32)
        ident = sb("ident", [P, P], F32)
        identb = sb("identb", [P, P], BF16)
        s12 = sb("s12", [P, MT, 2], F32)
        s2m = sb("s2m", [P, 2], F32)
        st = sb("st", [P, NT, 6], F32)
        mv = sb("mv", [P, NT, 2], F32)
        rs = sb("rs", [P, 2, NT], F32)
        mhalf = sb("mhalf", [P, NT], F32)
        lift = sb("lift", [P, 1], F32)
        msm = sb("msm", [P, 6, NT], F32)
        lrz = sb("lrz", [P, NT], F32)
        x1s = Q[:, :, :, :].rearrange("p a b c -> p (a b c)").bitcast(F32).rearrange(
            "p (b t f) -> p b t f", b=NB, t=NT)
        k1f = K1[:, :, :].rearrange("p a b -> p (a b)").bitcast(F32)
        k2f = K2[:, :, :].rearrange("p a b -> p (a b)").bitcast(F32)
        s1b = k1f[:, 0:N]
        mb = k1f[:, N:2 * N]
        run = k2f[:, 0:BLK]
        runs = [k2f[:, (2 + i) * BLK:(3 + i) * BLK] for i in range(2)]
        diag = k2f[:, BLK:2 * BLK].rearrange("p (t c) -> p t c", t=NT)
        ones = k2f[:, 4 * BLK:4 * BLK + P]
        pbf = probs[:, :, :, :].rearrange("p s i c -> p (s i c)").bitcast(BF16).rearrange(
            "p (s i c two) -> p s i c two", s=4, i=KT, two=2)[:, :, :, :, 1]
        Vp = V[:, :, :].rearrange("p m d -> p (m d)").bitcast(F16).rearrange(
            "p (m two h d) -> p m two h d", m=MT, two=2, h=H)
        vstage = r1
        adji = K1[:, :, :].rearrange("p a b -> p (a b)").bitcast(I32).rearrange("p (s n) -> p s n", s=2)
        adjb = K2[:, :, :].rearrange("p a b -> p (a b)").bitcast(BF16)[:, 0:2 * N].rearrange("p (s n) -> p s n", s=2)
        wst = Q[:, :, :, :].rearrange("p a b c -> p (a b c)").bitcast(F32)
        wnat = wst[:, 0:4 * FT * F].rearrange("p (w t f) -> p w t f", w=4, t=FT)
        w1f = wst[:, 2048:2048 + FT * (F + 2)].rearrange("p (t f) -> p t f", t=FT)
        abc = wst[:, 2600:2600 + 2 * F].rearrange("p (a f) -> p a f", a=2)
        wtmp = probs[:, 0, :, :].rearrange("p a c -> p (a c)").rearrange("p (a t f) -> p a t f", a=2, t=FT)

        S = ctx.enter_context(nc.psum_tensor("S", [P, 2, KT, BLK], F32))
        O = ctx.enter_context(nc.psum_tensor("O", [P, 2, BLK], F32))
        C = ctx.enter_context(nc.psum_tensor("C", [P, 2, BLK], F32))
        Sf = S[:, :, :, :].rearrange("p a b c -> p (a b) c")
        Sb = S[:, :, :, :].rearrange("p a b c -> p a (b c)").bitcast(BF16)
        Cn = C[:, :, :].rearrange("p a c -> p (a c)").rearrange("p (t f) -> p t f", t=NT)

        w_in, row_in, const_made = sem("w_in"), sem("row_in"), sem("const_made")
        wT_psum, wT_hi, wT_split = sem("wT_psum"), sem("wT_hi"), sem("wT_split")
        wa_made, w1_hi, w1_split, bias_made = sem("wa_made"), sem("w1_hi"), sem("w1_split"), sem("bias_made")
        adj_in = [sem("adj_in0"), sem("adj_in1")]
        adj_bf, adj_T, lim_act, lim_dve = sem("adj_bf"), sem("adj_T"), sem("lim_act"), sem("lim_dve")
        x_in, xT_psum, xT_hi, xT_split = sem("x_in"), sem("xT_psum"), sem("xT_hi"), sem("xT_split")
        q_psum, k_psum, v_psum = sem("q_psum"), sem("k_psum"), sem("v_psum")
        q_hi, k_hi, q_split, k_split = sem("q_hi"), sem("k_hi"), sem("q_split"), sem("k_split")
        k_swapped, v_made, v_ones = sem("k_swapped"), sem("v_made"), sem("v_ones")
        v_value, v_split, rest_made = sem("v_value"), sem("v_split"), sem("rest_made")
        pool_rest_made = sem("pool_rest_made")
        scored, clipped, exped, pv_done = sem("scored"), sem("clipped"), sem("exped"), sem("pv_done")
        o_read, rz_made, mult_done, summed = sem("o_read"), sem("rz_made"), sem("mult_done"), sem("summed")
        cT_psum, cT_hi, cT_split = sem("cT_psum"), sem("cT_hi"), sem("cT_split")
        res_in, res_bo, res_made = sem("res_in"), sem("res_bo"), sem("res_made")
        mix_psum, mix_read = sem("mix_psum"), sem("mix_read")
        ln_stats = [sem(f"ln{i}_stats") for i in range(3)]
        ln_mean = [sem(f"ln{i}_mean") for i in range(3)]
        ln_eps = [sem(f"ln{i}_eps") for i in range(3)]
        ln_rstd = [sem(f"ln{i}_rstd") for i in range(3)]
        ln_done = [sem(f"ln{i}_done") for i in range(3)]
        y_mult, y_made = sem("y_mult"), sem("y_made")
        x1_saved, x1T_psum, x1T_hi, x1T_split = sem("x1_saved"), sem("x1T_psum"), sem("x1T_hi"), sem("x1T_split")
        h_psum, h_read, h_ones = sem("h_psum"), sem("h_read"), sem("h_ones")
        s1b_psum, s1b_made, s12_made = sem("s1b_psum"), sem("s1b_made"), sem("s12_made")
        s2m_part, s2m_made = sem("s2m_part"), sem("s2m_made")
        run_step, run_T, max_step = sem("run_step"), sem("run_T"), sem("max_step")
        lmax, diag_made = sem("lmax"), sem("diag_made")
        mb_psum, mb_made = sem("mb_psum"), sem("mb_made")
        g_summed, g_leaky, g_masked, g_shifted, g_exped = sem("g_summed"), sem("g_leaky"), sem("g_masked"), sem("g_shifted"), sem("g_exped")
        g_used, acc_done, lrz_made, acc_read = sem("g_used"), sem("acc_done"), sem("lrz_made"), sem("acc_read")
        stored = sem("stored")
        waits_over = sem("waits_over")

        AHEAD = 1
        from_ahead = (xT_psum, y_made, summed, cT_psum, x1T_psum, x1_saved, acc_done, stored, mix_psum, adj_T, run_T,
                      lim_act, lim_dve, s1b_made, q_split, k_split, v_made, x1T_split, h_read, mb_made, acc_read, v_split, pv_done, k_swapped)

        block = ctx.enter_context(nc.Block())
        MAXSTEPS = 6
        RUN_AT = [4, 0, 3, 3, 4, 2]

        def blk(n):
            return bass.ts(n, BLK)

        def half(h):
            return slice(h * NT // 2, (h + 1) * NT // 2)

        def n_whole(last_block):
            return [] if last_block else [t for t in range(NT) if t // KT not in SPLIT]

        def rest_slot(h, j):
            return 2 if j == POOL_REST else (h * NREST + DVE_REST.index(j)) % 2

        def apart(eng):
            eng.sem_inc(waits_over, 1)

        def bcast(i):
            return rows[:, i, :].unsqueeze(1).to_broadcast([P, NT // 2, F])

        def y_gamma(eng, g, h):
            eng.wait_ge(ln_done[0], g * 2 + h + 1)
            eng.tensor_tensor(r1[:, half(h), :], r1[:, half(h), :], bcast(2), ALU.mult).then_inc(y_mult, 1)

        def y_residual(eng, g, h):
            eng.wait_ge(y_mult, g * 2 + h + 1)
            eng.wait_ge(res_made, g * 2 + h + 1)
            eng.tensor_tensor(r1[:, half(h), :], r1[:, half(h), :], xres[:, half(h), :], ALU.add).then_inc(y_made, 1)

        Y_STEPS = (17, 19, 20, 21)

        @block.sync
        def _(sp):
            for i, w in enumerate((Wq, Wk, Wv, Wo)):
                sp.dma_start(wnat[:, i, :, :], w.rearrange("(t p) f -> p t f", p=P)).then_inc(w_in, 16)
            sp.dma_start(w1f[:, :, 0:F], W1.rearrange("(t p) f -> p t f", p=P)).then_inc(w_in, 16)
            for i, r in enumerate((bv, bo, gamma, beta)):
                sp.dma_start(rows[:, i, :], r.rearrange("(a f) -> a f", a=1).to_broadcast([P, F])).then_inc(row_in, 16)
            for i in range(2):
                sp.dma_start(abc[:, i, :], a1[i * F:(i + 1) * F, :].rearrange("f a -> a f").to_broadcast([P, F])).then_inc(row_in, 16)
            for i, r in enumerate((bq, bk)):
                sp.dma_start(bqk[:, i, :], r.rearrange("(t p) -> p t", p=P), allow_slow_non_contiguous=True).then_inc(row_in, 16)
            adj_v = adj.rearrange("(t p) m -> t p m", p=P)
            for s in range(2):
                sp.dma_start(adji[:, s, :], adj_v[s]).then_inc(adj_in[s], 16)
            with sp.Fori(1, MT // 2) as i:
                for s in range(2):
                    sp.wait_ge(adj_bf, i * 2 + s - 1)
                    sp.dma_start(adji[:, s, :], adj_v[i * 2 + s]).then_inc(adj_in[s], 16)

            x_v = x.rearrange("b (k t p) f -> (b k) p t f", t=NT, p=P)
            out_v = out.rearrange("b (k t p) f -> (b k) p t f", t=NT, p=P)
            halves = (slice(0, 64), slice(64, 128))

            def load_x(b, n, again=False):
                sp.wait_ge(xT_psum, b * NB + n + AHEAD)
                sp.dma_start(xin[:, :, :], x_v[0 if again else b * NB + n]).then_inc(x_in, 16)

            def store(b, n):
                sp.wait_ge(ln_done[2], (b * NB + n + 1) * 2)
                sp.dma_start(out_v[b * NB + n], x1t[:, :, :]).then_inc(stored, 16)

            def swap_k(b, n):
                sp.wait_ge(k_split, b * NB + n + 1 + AHEAD)
                sp.wait_ge(k_swapped, (b * NB + n) * 32 + AHEAD)
                for i in range(2):
                    sp.dma_start(K2[halves[i], :, blk(n)], K1[halves[1 - i], :, blk(n)]).then_inc(k_swapped, 16)

            def batch(b, last):
                with sp.Fori(0, NB - 2) as n:
                    load_x(b, n + 2)
                    swap_k(b, n)
                with sp.Fori(NB - 2, NB) as n:
                    swap_k(b, n)
                sp.wait_ge(xT_psum, (b + 1) * NB + AHEAD)
                apart(sp)
                with sp.Fori(0, NB) as n:
                    sp.wait_ge(y_made, (b * NB + n) * 2 + AHEAD)
                    sp.dma_start(xres[:, :, :], x_v[b * NB + n]).then_inc(res_in, 16)
                    sp.wait_ge(ln_done[1], (b * NB + n + 1) * 2)
                    sp.dma_start(x1s[:, n, :, :], x1t[:, :, :]).then_inc(x1_saved, 16)
                load_x(b + 1, 0, again=last)
                with sp.Fori(0, NB - 1) as n:
                    store(b, n)
                if not last:
                    load_x(b + 1, 1)
                store(b, NB - 1)

            load_x(0, 0)
            load_x(0, 1)
            with sp.Fori(0, B - 1) as b:
                batch(b, False)
            batch(B - 1, True)
            sp.wait_ge(stored, B * NB * 16 + AHEAD)

        @block.gpsimd
        def _(pool):
            for s in from_ahead:
                pool.sem_inc(s, AHEAD)
            pool.memset(ident[:, :], 0.0).then_inc(const_made, 1)
            pool.memset(identb[:, :], 0.0).then_inc(const_made, 1)
            pool.memset(mhalf[:, :], -0.5).then_inc(const_made, 1)
            pool.memset(lift[:, :], LIFT).then_inc(const_made, 1)
            pool.wait_ge(const_made, 4)
            for m in (ident, identb):
                pool.affine_select(out=m[:, :], in_=m[:, :], compare_op=ALU.not_equal, fill=1.0,
                                   base=0, pattern=[[-1, P]], channel_multiplier=1).then_inc(const_made, 1)

            def rstd(kind, g):
                pool.wait_ge(ln_mean[kind], g + 1)
                apart(pool)
                pool.tensor_scalar(rs[:, 0, :], mv[:, :, 1], EPS, None, ALU.add).then_inc(ln_eps[kind], 1)
                pool.wait_ge(ln_eps[kind], g + 1)
                pool.tensor_tensor(rs[:, 1, :], rs[:, 0, :], mhalf[:, :], ALU.pow).then_inc(ln_rstd[kind], 1)

            def accumulate(b, n, s, head=False):
                t = b * TB + n * STEPS + s
                h, j, slot = s // CH, s % CH, s % 4
                dst = ctxs[:, :, h * DH:(h + 1) * DH]
                first = j == 0
                pool.wait_ge(summed, t + AHEAD)
                pool.wait_ge(rz_made, t + 1)
                if first and h == 0 and not head:
                    pool.wait_ge(cT_psum, (b * NB + n) * 2 - 1 + AHEAD)
                if first and h == 2:
                    pool.wait_ge(cT_psum, (b * NB + n) * 2 + AHEAD)
                o = pool.tensor_tensor(dst if first else scaled[:, :, :], osb[:, slot, :, 0:DH],
                                       rz[:, slot, :].unsqueeze(2).to_broadcast([P, NT, DH]), ALU.mult)
                if first:
                    o.then_inc(summed, 1)
                else:
                    o.then_inc(mult_done, 1)
                    pool.wait_ge(mult_done, (b * NB + n) * (STEPS - H) + s - h)
                    pool.tensor_tensor(dst, dst, scaled[:, :, :], ALU.add).then_inc(summed, 1)

            def rest(b, n, s):
                pool.wait_ge(exped, b * TB + n * STEPS + s + 1)
                pool.tensor_tensor(prest[:, 2, :, :], probs[:, s % 4, :, :], pbf[:, s % 4, :, :],
                                   ALU.subtract).then_inc(pool_rest_made, 1)

            def residual_bo(g, h):
                if h == 0:
                    pool.wait_ge(res_in, (g + 1) * 16)
                    pool.wait_ge(x1T_psum, g + AHEAD)
                    pool.wait_ge(x1_saved, g * 16 + AHEAD)
                pool.tensor_tensor(x1t[:, half(h), :], xres[:, half(h), :], bcast(1), ALU.add).then_inc(res_bo, 1)

            def residual_beta(g, h):
                pool.wait_ge(res_bo, g * 2 + h + 1)
                pool.tensor_tensor(xres[:, half(h), :], xres[:, half(h), :], bcast(3), ALU.add).then_inc(res_made, 1)

            pool_mix = {2: lambda g: residual_bo(g, 0), 4: lambda g: residual_bo(g, 1),
                        10: lambda g: residual_beta(g, 0), 12: lambda g: residual_beta(g, 1),
                        14: lambda g: rstd(0, g),
                        17: lambda g: y_gamma(pool, g, 0), 19: lambda g: y_gamma(pool, g, 1),
                        20: lambda g: y_residual(pool, g, 0), 21: lambda g: y_residual(pool, g, 1),
                        25: lambda g: rstd(1, g)}

            def attend(b, n, first):
                for s in range(STEPS):
                    if s >= 1 and (s - 1) % CH == POOL_REST:
                        rest(b, n, s - 1)
                    elif not first and s == 0:
                        rest(b, n - 1, STEPS - 1)
                    if s > LAG:
                        accumulate(b, n, s - LAG - 1, head=first)
                    elif not first:
                        accumulate(b, n - 1, STEPS + s - LAG - 1)
                    if not first and s in pool_mix:
                        pool_mix[s](b * NB + n - 1)

            def shift(b, n, j):
                k = b * NB * CH + n * CH + j
                pool.wait_ge(g_masked, k + 1)
                apart(pool)
                pool.tensor_tensor(probs[:, j % 4, :, :], probs[:, j % 4, :, :],
                                   mb[:, blk(n)].unsqueeze(1).to_broadcast([P, KT, BLK]),
                                   ALU.subtract).then_inc(g_shifted, 1)

            pool.wait_ge(row_in, 8 * 16)
            with pool.Fori(0, B) as b:
                pool.wait_ge(acc_done, b * NB * NT + AHEAD)
                vo = V[:, :, :].rearrange("p m (h d) -> p m h d", h=H)[:, :, :, DH]
                apart(pool)
                pool.memset(vo, 1.0).then_inc(v_ones, 1)
                pool.wait_ge(v_ones, b * 2 + 1)
                apart(pool)
                for j in SPLIT:
                    last = pool.memset(Vp[:, j * KT:(j + 1) * KT, 0, :, DH], 1.0)
                last.then_inc(v_ones, 1)

                def split_v(n, last_block):
                    g = b * NB + n
                    pool.wait_ge(v_made, g + 1 + AHEAD)
                    tiles = NT - len(n_whole(last_block))
                    src = vstage[:, 0:tiles, :].rearrange("p t (h d) -> p t h d", h=H)
                    apart(pool)
                    for t in range(tiles):
                        last = pool.tensor_copy(Vp[:, n * NT + t, 0, :, 0:DH], src[:, t, :, :])
                    last.then_inc(v_value, 1)
                    pool.wait_ge(v_value, g + 1)
                    apart(pool)
                    for t in range(tiles):
                        last = pool.tensor_tensor(Vp[:, n * NT + t, 1, :, 0:DH], src[:, t, :, :],
                                                  Vp[:, n * NT + t, 0, :, 0:DH], ALU.subtract)
                    last.then_inc(v_split, 1)
                with pool.Fori(0, NB - 1) as n:
                    split_v(n, False)
                split_v(NB - 1, True)
                pool.wait_ge(stored, b * NB * 16 + AHEAD)
                attend(b, 0, True)
                with pool.Fori(1, NB) as n:
                    attend(b, n, False)
                for s in range(LAG + 1):
                    accumulate(b, NB - 1, STEPS + s - LAG - 1)
                for s in sorted(pool_mix):
                    if s not in Y_STEPS:
                        pool_mix[s](b * NB + NB - 1)
                pool.wait_ge(pv_done, (b + 1) * TB + AHEAD)
                apart(pool)
                pool.memset(V[:, :, 0:1], 1.0).then_inc(h_ones, 1)
                pool.memset(ones, 1.0).then_inc(h_ones, 1)
                pool.wait_ge(s2m_part, b + 1)
                apart(pool)
                pool.partition_all_reduce(s2m[:, 1:2], s2m[:, 0:1], P, RMAX).then_inc(s2m_made, 1)

                def gat(n, first):
                    pool.wait_ge(mb_made, b * NB + n + 1 + AHEAD)
                    for j in range(CH):
                        shift(b, n, j)
                        if j == 3 and not first:
                            rstd(2, b * NB + n - 1)
                gat(0, True)
                with pool.Fori(1, NB) as n:
                    gat(n, False)
                rstd(2, b * NB + NB - 1)

        @block.scalar
        def _(act):
            for i in range(4):
                act.wait_ge(wT_psum, i + 1)
                act.activation(WTh[:, i, :, :], Sf[:, i, :].rearrange("p (t f) -> p t f", t=FT), ACT.Copy, scale=WS).then_inc(wT_hi, 1)
            act.wait_ge(wa_made, 1)
            act.activation(W1h[:, :, :], w1f, ACT.Copy, scale=WS).then_inc(w1_hi, 1)
            act.activation(arh[:, :, :], w1f[:, :, F:F + 1].to_broadcast([P, FT, P]), ACT.Copy, scale=WS).then_inc(w1_hi, 1)
            with act.Fori(0, MT // 2) as i:
                act.wait_ge(adj_T, i * 2 + 1 + AHEAD)
                apart(act)
                act.activation(limit[:, :, bass.ds(i * (2 * P), P)], Sb[:, 0, :].rearrange("p (m c) -> p m c", m=MT),
                               ACT.Copy).then_inc(lim_act, 1)

            def split_hi(b, n):
                g = b * NB + n
                act.wait_ge(q_psum, g + 1)
                apart(act)
                for o in range(FT):
                    for r in range(2):
                        rr = slice(64 * r, 64 * r + 64)
                        last = act.activation(Q[rr, n, 2 * o + r, :], Sf[rr, o, :], ACT.Identity, bias=bqk[rr, 0, o:o + 1])
                last.then_inc(q_hi, 1)
                act.wait_ge(k_psum, g + 1)
                apart(act)
                for o in range(FT):
                    for r in range(2):
                        rr = slice(64 * r, 64 * r + 64)
                        last = act.activation(K1[rr, 2 * o + r, blk(n)], Sf[rr, 2 + o, :], ACT.Identity, bias=bqk[rr, 1, o:o + 1])
                last.then_inc(k_hi, 1)

            def xT_value(b, n):
                act.wait_ge(xT_psum, b * NB + n + 1 + AHEAD)
                apart(act)
                act.activation(xTh[:, :, blk(n)], C[:, :, :], ACT.Copy).then_inc(xT_hi, 1)

            def exps(b, n, s):
                t = b * TB + n * STEPS + s
                act.wait_ge(clipped, t + 1)
                act.activation(probs[:, s % 4, :, :], probs[:, s % 4, :, :], ACT.Exp,
                               scale=1.0 / SC, bias=lift[:, 0:1]).then_inc(exped, 1)

            def read_o(b, n, s, early=False):
                t = b * TB + n * STEPS + s
                act.wait_ge(pv_done, t + 1 + AHEAD)
                if not early:
                    act.wait_ge(summed, t - 3 + AHEAD)
                act.activation(osb[:, s % 4, :, :], O[:, s % 2, 0:NT * DV].rearrange("p (t d) -> p t d", t=NT), ACT.Copy).then_inc(o_read, 1)

            def mix_value(g, o):
                act.wait_ge(cT_psum, g * 2 + o + 1 + AHEAD)
                act.wait_ge(mix_psum, g * NT + AHEAD)
                act.activation(cTh[:, o, :], C[:, o, :], ACT.Copy).then_inc(cT_hi, 1)

            def x1T_value(b, n):
                act.wait_ge(x1T_psum, b * NB + n + 1 + AHEAD)
                apart(act)
                act.activation(xTh[:, :, blk(n)], C[:, :, :], ACT.Copy).then_inc(x1T_hi, 1)

            def read_h(b, n):
                for i in range(NT):
                    act.wait_ge(h_psum, (b * NB + n) * NT + i + 1)
                    apart(act)
                    act.activation(V[:, n * NT + i, 1:F + 3], Sf[:, i, 0:F + 2], ACT.Copy, scale=1.0 / WS).then_inc(h_read, 1)
                act.wait_ge(s1b_psum, b * NB + n + 1)
                apart(act)
                act.activation(s1b[:, blk(n)], O[:, 0, :], ACT.Copy, scale=GS / WS).then_inc(s1b_made, 1)

            def attend(b, n, first):
                for s in range(STEPS):
                    exps(b, n, s)
                    if s >= LAG:
                        read_o(b, n, s - LAG, early=first and s < LAG + 4)
                    elif not first:
                        read_o(b, n - 1, STEPS + s - LAG)
                    if s in (3, 6) and not first:
                        mix_value(b * NB + n - 1, s // 6)
                    if s == 30 and not first:
                        x1T_value(b, n - 1)

            def pair_sum(b, n, j, early):
                if not early:
                    if j < 3:
                        act.wait_ge(g_used, (b * NB + n - 1) * (CH - 1) + j + 5)
                    elif j == 3:
                        act.wait_ge(acc_done, (b * NB + n) * NT + AHEAD)
                    else:
                        act.wait_ge(g_used, (b * NB + n) * (CH - 1) + j - 3)
                elif j > 3:
                    act.wait_ge(g_used, (b * NB + n) * (CH - 1) + j - 3)
                apart(act)
                for i in range(KT):
                    m = j * KT + i
                    last = act.activation(probs[:, j % 4, i, :], s1b[:, blk(n)], ACT.Identity, bias=s12[:, m, 1:2])
                last.then_inc(g_summed, 1)

            def read_mb(b, n):
                act.wait_ge(mb_psum, b * NB + n + 1)
                apart(act)
                act.activation(mb[:, blk(n)], O[:, 1, :], ACT.Copy).then_inc(mb_made, 1)

            def gat(b, n, first, last):
                for j in range(CH):
                    if j + 2 < CH:
                        pair_sum(b, n, j + 2, first)
                    elif not last:
                        pair_sum(b, n + 1, j + 2 - CH, False)
                    if j == CH - 1 and not last:
                        read_mb(b, n + 1)
                    if last and j == 4:
                        xT_value(b + 1, 0)
                    k = (b * NB + n) * CH + j
                    act.wait_ge(g_shifted, k + 1)
                    act.activation(probs[:, j % 4, :, :], probs[:, j % 4, :, :], ACT.Exp, scale=1.0 / GS).then_inc(g_exped, 1)

            act.wait_ge(bias_made, 1)
            act.wait_ge(const_made, 6)
            xT_value(0, 0)
            with act.Fori(0, B) as b:
                with act.Fori(0, NB - 1) as n:
                    xT_value(b, n + 1)
                    split_hi(b, n)
                split_hi(b, NB - 1)
                attend(b, 0, True)
                with act.Fori(1, NB) as n:
                    attend(b, n, False)
                for s in range(LAG):
                    read_o(b, NB - 1, STEPS + s - LAG)
                mix_value(b * NB + NB - 1, 0)
                read_h(b, 0)
                mix_value(b * NB + NB - 1, 1)
                with act.Fori(1, NB - 1) as n:
                    read_h(b, n)
                x1T_value(b, NB - 1)
                read_h(b, NB - 1)
                act.wait_ge(s1b_made, (b + 1) * NB + AHEAD)
                act.wait_ge(s12_made, b * 2 + 2)
                for j in range(2):
                    pair_sum(b, 0, j, True)
                read_mb(b, 0)
                gat(b, 0, True, False)
                with act.Fori(1, NB - 1) as n:
                    gat(b, n, False, False)
                gat(b, NB - 1, False, True)

        @block.vector
        def _(dve):
            for i in range(4):
                dve.wait_ge(wT_hi, i + 1)
                dve.scalar_tensor_tensor(WTl[:, i, :, :], Sf[:, i, :].rearrange("p (t f) -> p t f", t=FT), WS, WTh[:, i, :, :],
                                         ALU.mult, ALU.subtract).then_inc(wT_split, 1)
            dve.wait_ge(w_in, 5 * 16)
            dve.wait_ge(row_in, 8 * 16)
            for t in range(FT):
                for i in range(2):
                    last = dve.tensor_tensor(wtmp[:, i, t, :], w1f[:, t, 0:F], abc[:, i, :], ALU.mult)
            last.then_inc(run_step, 1)
            dve.wait_ge(run_step, 1)
            for i in range(2):
                last = dve.tensor_reduce(w1f[:, :, F + i], wtmp[:, i, :, :], AX.X, ALU.add)
            last.then_inc(wa_made, 1)
            dve.tensor_scalar(bqk[:, :, :], bqk[:, :, :], WS, None, ALU.mult).then_inc(bias_made, 1)
            dve.wait_ge(w1_hi, 2)
            dve.scalar_tensor_tensor(W1l[:, :, :], w1f, WS, W1h[:, :, :], ALU.mult, ALU.subtract).then_inc(w1_split, 1)
            dve.scalar_tensor_tensor(arl[:, :, :], w1f[:, :, F:F + 1].to_broadcast([P, FT, P]), WS, arh[:, :, :],
                                     ALU.mult, ALU.subtract).then_inc(w1_split, 1)

            def to_limit(i, s):
                dve.wait_ge(adj_in[s], i * 16 + 16)
                dve.wait_ge(adj_T, i * 2 + AHEAD)
                dve.tensor_scalar(adjb[:, s, :], adji[:, s, :], 2 * CLIP, -CLIP, ALU.mult, ALU.add).then_inc(adj_bf, 1)

            with dve.Fori(0, MT // 2) as i:
                to_limit(i, 0)
                to_limit(i, 1)
                dve.wait_ge(adj_T, i * 2 + 2 + AHEAD)
                dve.tensor_copy(limit[:, :, bass.ds(i * (2 * P) + P, P)], Sb[:, 1, :].rearrange("p (m c) -> p m c", m=MT)).then_inc(lim_dve, 1)

            def xT_rest(b, n):
                dve.wait_ge(xT_hi, b * NB + n + 1)
                dve.tensor_tensor(xTl[:, :, blk(n)], C[:, :, :], xTh[:, :, blk(n)], ALU.subtract).then_inc(xT_split, 1)

            def split_rest(b, n, last_block=False):
                g = b * NB + n
                for w, ready, done in ((0, q_hi, q_split), (1, k_hi, k_split)):
                    dve.wait_ge(ready, g + 1)
                    for o in range(FT):
                        for r in range(2):
                            rr = slice(64 * r, 64 * r + 64)
                            ll = slice(64 - 64 * r, 128 - 64 * r)
                            val = (lambda s: Q[s, n, 2 * o + r, :] if w == 0 else K1[s, 2 * o + r, blk(n)])
                            last = dve.scalar_tensor_tensor(val(ll), Sf[rr, 2 * w + o, :], bqk[rr, w, o:o + 1], val(rr),
                                                            ALU.add, ALU.subtract)
                    last.then_inc(done, 1)
                dve.wait_ge(v_psum, g + 1)
                dve.wait_ge(v_split, g + AHEAD)
                apart(dve)
                whole = n_whole(last_block)
                for t in range(NT):
                    dst = (V[:, n * NT + t, :].rearrange("p (h d) -> p h d", h=H)[:, :, 0:DH] if t in whole else
                           vstage[:, t, :].rearrange("p (h d) -> p h d", h=H))
                    last = dve.scalar_tensor_tensor(
                        dst, O[:, t // 2, (t % 2) * F:(t % 2 + 1) * F].rearrange("p (h d) -> p h d", h=H), 1.0 / WS,
                        rows[:, 0, :].rearrange("p (h d) -> p h d", h=H), ALU.mult, ALU.add)
                last.then_inc(v_made, 1)

            def clip(b, n, s):
                t = b * TB + n * STEPS + s
                j = s % CH
                dve.wait_ge(scored, t + 1)
                dve.scalar_tensor_tensor(probs[:, s % 4, :, :], S[:, s % 2, :, :], -CLIP,
                                         limit[:, j * KT:(j + 1) * KT, blk(n)], ALU.max, ALU.min).then_inc(clipped, 1)

            def rest(b, n, s, first=False):
                t = b * TB + n * STEPS + s
                h, j = s // CH, s % CH
                if j in DVE_REST:
                    dve.wait_ge(exped, t + 1)
                    if not (first and h * NREST + DVE_REST.index(j) < 2):
                        dve.wait_ge(pv_done, t - 3 + AHEAD)
                    dve.tensor_tensor(prest[:, rest_slot(h, j), :, :], probs[:, s % 4, :, :], pbf[:, s % 4, :, :],
                                      ALU.subtract).then_inc(rest_made, 1)

            def recip(b, n, s):
                t = b * TB + n * STEPS + s
                dve.wait_ge(o_read, t + 1)
                dve.reciprocal(rz[:, s % 4, :], osb[:, s % 4, :, DH]).then_inc(rz_made, 1)

            def stats(kind, h):
                for t in range(NT)[half(h)]:
                    last = dve.bn_stats(st[:, t, :], r1[:, t, :])
                last.then_inc(ln_stats[kind], 1)

            def mean(kind, g):
                dve.wait_ge(ln_stats[kind], (g + 1) * 2)
                apart(dve)
                for t in range(NT):
                    last = dve.bn_aggr(mv[:, t, :], st[:, t, :])
                last.then_inc(ln_mean[kind], 1)

            def normalise(kind, g, h, dst):
                if h == 0:
                    dve.wait_ge(ln_rstd[kind], g + 1)
                for t in range(NT)[half(h)]:
                    last = dve.tensor_scalar(dst[:, t, :], r1[:, t, :], mv[:, t, 0:1], rs[:, 1, t:t + 1], ALU.subtract, ALU.mult)
                last.then_inc(ln_done[kind], 1)

            def mix_rest(g, o):
                dve.wait_ge(cT_hi, g * 2 + o + 1)
                dve.tensor_tensor(cTl[:, o, :], C[:, o, :], cTh[:, o, :], ALU.subtract).then_inc(cT_split, 1)

            def mix_add(g, h):
                dve.wait_ge(mix_psum, g * NT + (h + 1) * NT // 2 + AHEAD)
                dve.wait_ge(res_bo, g * 2 + h + 1)
                dve.scalar_tensor_tensor(r1[:, half(h), :], Cn[:, half(h), :], 1.0 / WS, x1t[:, half(h), :],
                                         ALU.mult, ALU.add).then_inc(mix_read, 1)

            def mix_stats1(g, h):
                dve.wait_ge(mix_read, g * 2 + h + 1)
                stats(0, h)

            def mix_stats2(g, h):
                dve.wait_ge(y_made, g * 2 + h + 1 + AHEAD)
                stats(1, h)

            dve_mix = {4: lambda g: mix_rest(g, 0), 7: lambda g: mix_rest(g, 1),
                       10: lambda g: mix_add(g, 0), 11: lambda g: mix_stats1(g, 0),
                       12: lambda g: mix_add(g, 1), 13: lambda g: mix_stats1(g, 1), 14: lambda g: mean(0, g),
                       16: lambda g: normalise(0, g, 0, r1), 17: lambda g: normalise(0, g, 1, r1),
                       22: lambda g: mix_stats2(g, 0), 23: lambda g: mix_stats2(g, 1), 24: lambda g: mean(1, g),
                       27: lambda g: normalise(1, g, 0, x1t), 28: lambda g: normalise(1, g, 1, x1t)}

            def x1T_rest(b, n):
                dve.wait_ge(x1T_hi, b * NB + n + 1)
                dve.tensor_tensor(xTl[:, :, blk(n)], C[:, :, :], xTh[:, :, blk(n)], ALU.subtract).then_inc(x1T_split, 1)

            def attend(b, n, first):
                for s in range(STEPS):
                    clip(b, n, s)
                    if s >= 1:
                        rest(b, n, s - 1, first)
                    elif not first:
                        rest(b, n - 1, STEPS - 1)
                    if s > LAG:
                        recip(b, n, s - LAG - 1)
                    elif not first:
                        recip(b, n - 1, STEPS + s - LAG - 1)
                    if not first and s in dve_mix:
                        dve_mix[s](b * NB + n - 1)
                    if not first and s == STEPS - 1:
                        x1T_rest(b, n - 1)

            def run_max(b, n, m):
                before = (b * NB + n) * (MT + 1) + 1
                r = runs[m % 2]
                if m < 2:
                    dve.wait_ge(run_T, b * NB + n + AHEAD)
                    dve.wait_ge(run_step, before)
                    dve.tensor_scalar(r, limit[:, m, blk(n)], s12[:, m, 1:2], None, ALU.min).then_inc(run_step, 1)
                else:
                    dve.wait_ge(run_step, before + m - 1)
                    dve.scalar_tensor_tensor(r, limit[:, m, blk(n)], s12[:, m, 1:2], r, ALU.min, ALU.max).then_inc(run_step, 1)
                if m == MT - 1:
                    dve.wait_ge(run_step, before + MT)
                    dve.tensor_tensor(run, runs[0], runs[1], ALU.max).then_inc(run_step, 1)

            def node_scores(b, m0, m1):
                dve.wait_ge(h_read, b * MT + m1 + AHEAD)
                dve.tensor_scalar(s12[:, m0:m1, :], V[:, m0:m1, F + 1:F + 3], GS, None, ALU.mult).then_inc(s12_made, 1)
                dve.wait_ge(s12_made, b * 2 + (2 if m1 == MT else 1))

            def row_max(b, n):
                g = b * NB + n
                G, some, cand, sel, lk, M = (msm[:, i, :] for i in range(6))
                steps = [0]

                def link(o):
                    steps[0] += 1
                    o.then_inc(max_step, 1)
                    dve.wait_ge(max_step, g * MAXSTEPS + steps[0])

                dve.wait_ge(run_T, g + 1 + AHEAD)
                link(dve.tensor_reduce(G, O[:, 0, :].rearrange("p (t c) -> p t c", t=NT), AX.X, ALU.max))
                link(dve.tensor_scalar(some, G, -CLIP, None, ALU.is_gt))
                link(dve.scalar_tensor_tensor(cand, some, -2.0 ** 60, s2m[:, 1:2].to_broadcast([P, NT]), ALU.mult, ALU.add))
                link(dve.tensor_tensor(sel, G, cand, ALU.max))
                link(dve.tensor_tensor(lk, s12[:, bass.ts(n, NT), 0], sel, ALU.add))
                dve.tensor_scalar(some, some, CLIP, -CLIP, ALU.mult, ALU.add)
                link(dve.scalar_tensor_tensor(M, lk, SLOPE, lk, ALU.mult, ALU.max))
                dve.tensor_tensor(M, M, some, ALU.add).then_inc(lmax, 1)
                dve.wait_ge(lmax, g + 1)
                dve.tensor_tensor(diag, ident[:, :].unsqueeze(1).to_broadcast([P, NT, P]),
                                  M.unsqueeze(2).to_broadcast([P, NT, P]), ALU.mult).then_inc(diag_made, 1)

            def finish(b, n):
                g = b * NB + n
                for t in range(NT):
                    dve.wait_ge(acc_done, g * NT + t + 1 + AHEAD)
                    dve.reciprocal(lrz[:, t:t + 1], Sf[:, t, 0:1]).then_inc(lrz_made, 1)
                for t in range(NT):
                    dve.wait_ge(lrz_made, g * NT + t + 1)
                    dve.scalar_tensor_tensor(r1[:, t, :], Sf[:, t, 1:F + 1], lrz[:, t:t + 1], x1s[:, n, t, :],
                                             ALU.mult, ALU.add).then_inc(acc_read, 1)

            def finish_stats(g):
                dve.wait_ge(acc_read, (g + 1) * NT + AHEAD)
                for h in range(2):
                    stats(2, h)

            def finish_norm(g):
                dve.wait_ge(stored, g * 16 + AHEAD)
                for h in range(2):
                    normalise(2, g, h, x1t)

            def gat(b, n, first, last):
                m = 0
                for j in range(CH):
                    k = (b * NB + n) * CH + j
                    w = probs[:, j % 4, :, :]
                    dve.wait_ge(g_summed, k + 1)
                    dve.scalar_tensor_tensor(w, w, SLOPE, w, ALU.mult, ALU.max).then_inc(g_leaky, 1)
                    runs_now = 0 if last or j >= len(RUN_AT) else RUN_AT[j]
                    if runs_now:
                        run_max(b, n + 1, m)
                        m += 1
                    dve.wait_ge(g_leaky, k + 1)
                    dve.scalar_tensor_tensor(w, limit[:, j * KT:(j + 1) * KT, blk(n)], 0.0,
                                             w, ALU.min, ALU.add).then_inc(g_masked, 1)
                    if not first:
                        if j == 1:
                            finish(b, n - 1)
                        if j == 2:
                            finish_stats(b * NB + n - 1)
                        if j == 3:
                            mean(2, b * NB + n - 1)
                        if j == CH - 1:
                            finish_norm(b * NB + n - 1)
                    for _ in range(runs_now - 1):
                        run_max(b, n + 1, m)
                        m += 1
                    if not last and j == 6:
                        row_max(b, n + 1)
                    if last and j == 5:
                        xT_rest(b + 1, 0)

            xT_rest(0, 0)
            with dve.Fori(0, B) as b:
                with dve.Fori(0, NB - 1) as n:
                    xT_rest(b, n + 1)
                    split_rest(b, n)
                split_rest(b, NB - 1, True)
                attend(b, 0, True)
                with dve.Fori(1, NB) as n:
                    attend(b, n, False)
                dve.wait_ge(exped, (b + 1) * TB)
                dve.tensor_tensor(prest[:, 2, :, :], probs[:, (STEPS - 1) % 4, :, :], pbf[:, (STEPS - 1) % 4, :, :],
                                  ALU.subtract).then_inc(pool_rest_made, 1)
                for s in range(LAG + 1):
                    recip(b, NB - 1, STEPS + s - LAG - 1)
                last_g = b * NB + NB - 1
                early = (NB - 1) * NT
                for s in sorted(dve_mix):
                    if s == 22:
                        for h in range(2):
                            y_gamma(dve, last_g, h)
                        for h in range(2):
                            y_residual(dve, last_g, h)
                    if s == 27:
                        node_scores(b, 0, early)
                        for m in range(2):
                            run_max(b, 0, m)
                    dve_mix[s](last_g)
                for m in range(2, early // 2):
                    run_max(b, 0, m)
                x1T_rest(b, NB - 1)
                for m in range(early // 2, early):
                    run_max(b, 0, m)
                node_scores(b, early, MT)
                dve.tensor_reduce(s2m[:, 0:1], s12[:, :, 1], AX.X, ALU.max).then_inc(s2m_part, 1)
                for m in range(early, MT):
                    run_max(b, 0, m)
                dve.wait_ge(x1_saved, (b + 1) * NB * 16 + AHEAD)
                dve.wait_ge(s2m_made, b + 1)
                row_max(b, 0)
                gat(b, 0, True, False)
                with dve.Fori(1, NB - 1) as n:
                    gat(b, n, False, False)
                gat(b, NB - 1, False, True)
                finish(b, NB - 1)
                finish_stats(b * NB + NB - 1)
                mean(2, b * NB + NB - 1)
                finish_norm(b * NB + NB - 1)
                dve.wait_ge(ln_done[2], (b + 1) * NB * 2)

        @block.tensor
        def _(pe):
            pe.wait_ge(const_made, 6)
            pe.wait_ge(w_in, 5 * 16)
            for i in range(4):
                for ft in range(FT):
                    for ot in range(FT):
                        last = pe.transpose(Sf[:, i, ft * F + ot * P:ft * F + (ot + 1) * P], wnat[:, i, ot, ft * P:(ft + 1) * P], ident[:, :])
                last.then_inc(wT_psum, 1)
            pe.wait_ge(wT_split, 4)
            with pe.Fori(0, MT // 2) as i:
                for s, lim in ((0, lim_act), (1, lim_dve)):
                    pe.wait_ge(adj_bf, i * 2 + s + 1)
                    pe.wait_ge(lim, i + AHEAD)
                    for m in range(MT):
                        last = pe.transpose(Sb[:, s, m * P:(m + 1) * P], adjb[:, s, m * P:(m + 1) * P], identb[:, :])
                    last.then_inc(adj_T, 1)

            def split_mm(dst, pairs):
                ops = [(lh, rh) for (lh, ll, rh, rl) in pairs] + [(lh, rl) for (lh, ll, rh, rl) in pairs] + \
                      [(ll, rh) for (lh, ll, rh, rl) in pairs]
                for i, (w, m) in enumerate(ops):
                    last = pe.matmul(dst, lhsT=w, rhs=m, start=i == 0, stop=i == len(ops) - 1)
                return last

            def xT(b, n, head):
                g = b * NB + n
                pe.wait_ge(x_in, g * 16 + 16)
                if not head:
                    pe.wait_ge(xT_split, g)
                for ft in range(FT):
                    for t in range(NT):
                        last = pe.transpose(C[:, ft, t * P:(t + 1) * P], xin[:, t, ft * P:(ft + 1) * P], ident[:, :])
                last.then_inc(xT_psum, 1)

            def qkv(b, n, head):
                g = b * NB + n
                pe.wait_ge(xT_split, g + 1)
                for w, psum, free in ((0, q_psum, q_split), (1, k_psum, k_split)):
                    pe.wait_ge(free, g + AHEAD)
                    if w == 0:
                        pe.wait_ge(acc_read, b * MT + AHEAD)
                    for o in range(FT):
                        last = split_mm(Sf[:, 2 * w + o, :], [
                            (WTh[:, w, ft, o * P:(o + 1) * P], WTl[:, w, ft, o * P:(o + 1) * P],
                             xTh[:, ft, blk(n)], xTl[:, ft, blk(n)]) for ft in range(FT)])
                    last.then_inc(psum, 1)
                pe.wait_ge(v_made, g + AHEAD)
                for t in range(NT):
                    cols = bass.ds(n * BLK + t * P, P)
                    last = split_mm(O[:, t // 2, (t % 2) * F:(t % 2 + 1) * F], [
                        (xTh[:, ft, cols], xTl[:, ft, cols], WTh[:, 2, ft, :], WTl[:, 2, ft, :]) for ft in range(FT)])
                last.then_inc(v_psum, 1)

            def score(b, n, s, head=False):
                t = b * TB + n * STEPS + s
                h, j = s // CH, s % CH
                if isinstance(n, int) and h == 0 and j * KT % NT == 0:
                    pe.wait_ge(k_swapped, (b * NB + j * KT // NT + 1) * 32 + AHEAD)
                if not head:
                    pe.wait_ge(clipped, t - 1)
                for i in range(KT):
                    m = j * KT + i
                    for r, K in enumerate((K1, K2)):
                        last = pe.matmul(S[:, s % 2, i, :], lhsT=K[:, h, m * P:(m + 1) * P], rhs=Q[:, n, h, :],
                                         start=r == 0, stop=r == 1)
                last.then_inc(scored, 1)

            def pv(b, n, s, head=False):
                t = b * TB + n * STEPS + s
                h, j = s // CH, s % CH
                if isinstance(n, int) and h == 0 and j * KT % NT == 0:
                    pe.wait_ge(v_split, b * NB + j * KT // NT + 1 + AHEAD)
                if j == POOL_REST:
                    pe.wait_ge(pool_rest_made, (b * NB + n) * H + h + 1)
                elif j in SPLIT:
                    pe.wait_ge(rest_made, ((b * NB + n) * H + h) * NREST + DVE_REST.index(j) + 1)
                else:
                    pe.wait_ge(exped, t + 1)
                if not head:
                    pe.wait_ge(o_read, t - 1)
                for q in range(NT):
                    cols = slice(q * P, (q + 1) * P)
                    for i in range(KT):
                        m = j * KT + i
                        o = O[:, s % 2, q * DV:(q + 1) * DV]
                        if j in SPLIT:
                            for r, w in enumerate((pbf[:, s % 4, i, cols], prest[:, rest_slot(h, j), i, cols])):
                                pe.matmul(o, lhsT=w, rhs=Vp[:, m, 0, h, :], start=i == 0 and r == 0, stop=False)
                                last = pe.matmul(o[:, 0:DH], lhsT=w, rhs=Vp[:, m, 1, h, 0:DH], start=False,
                                                 stop=i == KT - 1 and r == 1)
                        else:
                            last = pe.matmul(o, lhsT=probs[:, s % 4, i, cols], rhs=V[:, m, h * DV:(h + 1) * DV],
                                             start=i == 0, stop=i == KT - 1)
                last.then_inc(pv_done, 1)

            def mix_T(b, n, o):
                g = b * NB + n
                pe.wait_ge(summed, b * TB + n * STEPS + (o + 1) * STEPS // 2 + AHEAD)
                if o == 0:
                    pe.wait_ge(x1T_split, g + AHEAD)
                for t in range(NT):
                    last = pe.transpose(C[:, o, t * P:(t + 1) * P], ctxs[:, t, o * P:(o + 1) * P], ident[:, :])
                last.then_inc(cT_psum, 1)

            def mix_project(b, n, t):
                if t == 0:
                    pe.wait_ge(cT_split, (b * NB + n) * 2 + 2)
                split_mm(Cn[:, t, :], [
                    (cTh[:, o, t * P:(t + 1) * P], cTl[:, o, t * P:(t + 1) * P], WTh[:, 3, o, :], WTl[:, 3, o, :])
                    for o in range(FT)]).then_inc(mix_psum, 1)

            def x1T(b, n):
                pe.wait_ge(ln_done[1], (b * NB + n + 1) * 2)
                for ft in range(FT):
                    for t in range(NT):
                        last = pe.transpose(C[:, ft, t * P:(t + 1) * P], x1t[:, t, ft * P:(ft + 1) * P], ident[:, :])
                last.then_inc(x1T_psum, 1)

            pe_mix = {2: lambda b, n: mix_T(b, n, 0), 5: lambda b, n: mix_T(b, n, 1),
                      8: lambda b, n: mix_project(b, n, 0), 9: lambda b, n: mix_project(b, n, 1),
                      10: lambda b, n: mix_project(b, n, 2), 11: lambda b, n: mix_project(b, n, 3),
                      29: x1T}

            def attend(b, n, first):
                for s in range(STEPS):
                    if first and s == 1:
                        pe.wait_ge(k_split, (b + 1) * NB + AHEAD)
                    score(b, n, s, head=first and s < 2)
                    if first and s == LAG:
                        pe.wait_ge(v_made, (b + 1) * NB + AHEAD)
                        pe.wait_ge(v_ones, (b + 1) * 2)
                    if s >= LAG:
                        pv(b, n, s - LAG, head=first and s < LAG + 2)
                    elif not first:
                        pv(b, n - 1, STEPS + s - LAG)
                    if not first and s in pe_mix:
                        pe_mix[s](b, n - 1)

            def gat_sum(b, n, j, head):
                k = (b * NB + n) * CH + j
                pe.wait_ge(g_exped, k + 1)
                for q in range(NT):
                    if j == 0 and not head:
                        pe.wait_ge(acc_read, (b * NB + n - 1) * NT + q + 1 + AHEAD)
                    for i in range(KT):
                        last = pe.matmul(Sf[:, q, 0:F + 1], lhsT=probs[:, j % 4, i, q * P:(q + 1) * P],
                                         rhs=V[:, j * KT + i, 0:F + 1], start=j == 0 and i == 0,
                                         stop=j == CH - 1 and i == KT - 1)
                    if j == CH - 1:
                        last.then_inc(acc_done, 1)
                if j < CH - 1:
                    last.then_inc(g_used, 1)

            def run_transpose(b, n):
                pe.wait_ge(run_step, (b * NB + n + 1) * (MT + 1) + 1)
                for t in range(NT):
                    last = pe.transpose(O[:, 0, t * P:(t + 1) * P], run[:, t * P:(t + 1) * P], ident[:, :])
                last.then_inc(run_T, 1)

            def spread_max(b, n):
                pe.wait_ge(diag_made, b * NB + n + 1)
                pe.wait_ge(mb_made, b * NB + n + AHEAD)
                pe.matmul(O[:, 1, :], lhsT=ones, rhs=k2f[:, BLK:2 * BLK], start=True, stop=True).then_inc(mb_psum, 1)

            def gat(b, n, first, last):
                for j in range(CH):
                    if not last and j == 5:
                        run_transpose(b, n + 1)
                    if not last and j == 6:
                        spread_max(b, n + 1)
                    if last and j == 3:
                        xT(b + 1, 0, True)
                    gat_sum(b, n, j, first)

            def gat_h(b, n):
                pe.wait_ge(x1T_split, b * NB + n + 1 + AHEAD)
                for t in range(NT):
                    pe.wait_ge(h_read, (b * NB + n) * NT + AHEAD)
                    cols = bass.ds(n * BLK + t * P, P)
                    split_mm(Sf[:, t, 0:F + 2], [
                        (xTh[:, ft, cols], xTl[:, ft, cols], W1h[:, ft, :], W1l[:, ft, :]) for ft in range(FT)]
                    ).then_inc(h_psum, 1)
                pe.wait_ge(s1b_made, b * NB + n + AHEAD)
                pe.wait_ge(o_read, (b + 1) * TB)
                split_mm(O[:, 0, :], [
                    (arh[:, ft, :], arl[:, ft, :], xTh[:, ft, blk(n)], xTl[:, ft, blk(n)]) for ft in range(FT)]
                ).then_inc(s1b_psum, 1)

            pe.wait_ge(w1_split, 2)
            xT(0, 0, True)
            with pe.Fori(0, B) as b:
                with pe.Fori(0, NB - 1) as n:
                    xT(b, n + 1, False)
                    qkv(b, n, False)
                qkv(b, NB - 1, False)
                pe.wait_ge(q_split, (b + 1) * NB + AHEAD)
                pe.wait_ge(lim_act, MT // 2 + AHEAD)
                pe.wait_ge(lim_dve, MT // 2 + AHEAD)
                attend(b, 0, True)
                with pe.Fori(1, NB) as n:
                    attend(b, n, False)
                for s in range(LAG):
                    pv(b, NB - 1, STEPS + s - LAG)
                mix_T(b, NB - 1, 0)
                gat_h(b, 0)
                mix_T(b, NB - 1, 1)
                for t in range(NT):
                    mix_project(b, NB - 1, t)
                with pe.Fori(1, NB - 1) as n:
                    gat_h(b, n)
                x1T(b, NB - 1)
                gat_h(b, NB - 1)
                pe.wait_ge(s1b_made, (b + 1) * NB + AHEAD)
                run_transpose(b, 0)
                pe.wait_ge(h_ones, (b + 1) * 2)
                spread_max(b, 0)
                pe.wait_ge(h_read, (b + 1) * MT + AHEAD)
                gat(b, 0, True, False)
                with pe.Fori(1, NB - 1) as n:
                    gat(b, n, False, False)
                gat(b, NB - 1, False, True)


_INS = ["x", "adj", "L0_gnn_Wq", "L0_gnn_bq", "L0_gnn_Wk", "L0_gnn_bk", "L0_gnn_Wv", "L0_gnn_bv",
        "L0_gnn_Wo", "L0_gnn_bo", "L0_gnn_gamma", "L0_gnn_beta", "L1_gnn_W", "L1_gnn_a"]


def kernel(**inputs):
    import numpy as _np
    import concourse.bacc as _bacc
    from concourse import mybir as _mybir
    from concourse.bass_utils import run_bass_kernel_spmd as _run

    nc = _bacc.Bacc("TRN2", target_bir_lowering=False, num_devices=1)
    arrays, args = {}, []
    for name in _INS:
        a = _np.ascontiguousarray(inputs[name])
        arrays[f"in_{name}_dram"] = a
        args.append(nc.dram_tensor(f"in_{name}_dram", a.shape, _mybir.dt.from_np(a.dtype), kind="ExternalInput").ap())
    out = nc.dram_tensor("out_0_dram", inputs["x"].shape, _mybir.dt.float32, kind="ExternalOutput").ap()
    adj_resnorm_kernel(nc, *args, out)
    r = _run(nc, [arrays], core_ids=[0])
    return r.results[0]["out_0_dram"]
```
